# Optimizing a Trainium2 kernel written in Bass

```python
import numpy as np
import jax
import jax.numpy as jnp

def _softmax(x, axis=-1):
    return jax.nn.softmax(x, axis=axis)

def _gelu(x):
    return jax.nn.gelu(x, approximate=True)

def _silu(x):
    return jax.nn.silu(x)

def _sigmoid(x):
    return jax.nn.sigmoid(x)

def _layernorm(x, axis=-1, eps=1e-05):
    m = jnp.mean(x, axis=axis, keepdims=True)
    v = jnp.var(x, axis=axis, keepdims=True)
    return (x - m) / jnp.sqrt(v + eps)

def _scatter_add(tgt, idx, src, axis=0):
    return tgt.at[idx].add(src)

def _segment_sum(src, seg, n):
    return jax.ops.segment_sum(src, seg, n)
kernel_name = 'mk_seq_postln_d1_jaxref_r8_4c31f8'

def setup_inputs(seed: int=0):
    np.random.seed(seed)
    _w = jnp.asarray

    def _L0_attn_setup():
        import jax, jax.numpy as jnp
        import numpy as np
        NUM_HEAD = 16
        D_Q = 64
        D_KV = 64
        ROPE_BASE = 10000.0

        def _cos_sin(seq_len, dim):
            pos = jnp.arange(seq_len, dtype=jnp.float32)[:, None]
            ids = jnp.arange(dim // 2, dtype=jnp.float32)
            theta = ROPE_BASE ** (-2.0 * ids) / (dim // 2)
            r = pos * theta[None, :]
            return (jnp.cos(r), jnp.sin(r))

        def _rope(x, cos, sin):
            b, s, d = x.shape
            xv = x.reshape(b, s, d // 2, 2)
            x0, x1 = (xv[..., 0], xv[..., 1])
            out = jnp.stack([x0 * cos - x1 * sin, x1 * cos + x0 * sin], axis=-1)
            return out.reshape(b, s, d)
        key = jax.random.key(seed)
        ks = jax.random.split(key, 10)
        d_model, d_q, d_kv = (128, D_Q, D_KV)
        b, s = (2, 256)
        w = lambda k, i, o: jax.random.normal(k, (i, o), dtype=jnp.float32) * 0.02
        return {'x': jax.random.normal(ks[0], (b, s, d_model), dtype=jnp.float32), 'Wd_q_w': w(ks[1], d_model, d_q), 'Wd_q_b': jnp.zeros((d_q,), jnp.float32), 'Wu_q_w': w(ks[2], d_q, d_model), 'Wu_q_b': jnp.zeros((d_model,), jnp.float32), 'Wq_r_w': w(ks[3], d_q, d_model), 'Wq_r_b': jnp.zeros((d_model,), jnp.float32), 'Wk_r_w': w(ks[4], d_model, d_model), 'Wk_r_b': jnp.zeros((d_model,), jnp.float32), 'Wd_kv_w': w(ks[5], d_model, d_kv), 'Wd_kv_b': jnp.zeros((d_kv,), jnp.float32), 'Wu_k_w': w(ks[6], d_kv, d_model), 'Wu_k_b': jnp.zeros((d_model,), jnp.float32), 'Wu_v_w': w(ks[7], d_kv, d_model), 'Wu_v_b': jnp.zeros((d_model,), jnp.float32), 'Wo_w': w(ks[8], d_model, d_model), 'Wo_b': jnp.zeros((d_model,), jnp.float32)}
    _L0_attn_in = _L0_attn_setup()

    def _L0_ffn_setup():
        import jax, jax.numpy as jnp
        import numpy as np
        DIM = 128
        DEPTH = 6
        HEADS = 16
        DIM_HEAD = 64
        WINDOW = 32
        INNER = HEADS * DIM_HEAD
        DIM_INNER = int(DIM * 4 * 2 / 3)
        QK_SCALE = 8.0

        def shift_tokens(t):
            a, s = jnp.split(t, 2, -1)
            s = jnp.pad(s, ((0, 0), (1, 0), (0, 0)))[:, :-1]
            return jnp.concatenate([a, s], -1)

        def l2norm(t):
            return t / jnp.maximum(jnp.linalg.norm(t, axis=-1, keepdims=True), 1e-12)

        def rotate_half(x):
            x1, x2 = jnp.split(x, 2, -1)
            return jnp.concatenate([-x2, x1], -1)

        def rotary_tables(n):
            half = jnp.arange(0, DIM_HEAD, 2, dtype=jnp.float32)
            inv_freq = 1.0 / 10000.0 ** (half / DIM_HEAD)
            t = jnp.arange(n, dtype=jnp.float32)
            freqs = t[:, None] * inv_freq[None, :]
            freqs = jnp.concatenate([freqs, freqs], -1)
            base_scale = (half + 0.4 * DIM_HEAD) / (1.4 * DIM_HEAD)
            power = (t - n // 2) / (WINDOW // 2)
            scale = base_scale[None, :] ** power[:, None]
            scale = jnp.concatenate([scale, scale], -1)
            return (freqs, scale)

        def local_attention(q, k, v):
            b, h, n, d = q.shape
            w = WINDOW
            nw = n // w
            bq = q.reshape(b, h, nw, w, d)
            bk = k.reshape(b, h, nw, w, d)
            bv = v.reshape(b, h, nw, w, d)

            def look(t):
                p = jnp.pad(t, ((0, 0), (0, 0), (1, 0), (0, 0), (0, 0)))
                return jnp.concatenate([p[:, :, :nw], p[:, :, 1:]], axis=3)
            bk2, bv2 = (look(bk), look(bv))
            seq = jnp.arange(n).reshape(nw, w)
            seq_p = jnp.pad(seq, ((1, 0), (0, 0)), constant_values=-1)
            jt = jnp.concatenate([seq_p[:nw], seq_p[1:]], axis=1)
            it = seq[:, :, None]
            jb = jt[:, None, :]
            mask = (it < jb) | (it > jb + w) | (jb == -1)
            sim = jnp.einsum('bhwie,bhwje->bhwij', bq, bk2) * QK_SCALE
            sim = jnp.where(mask, -jnp.finfo(sim.dtype).max, sim)
            attn = jax.nn.softmax(sim, -1)
            out = jnp.einsum('bhwij,bhwje->bhwie', attn, bv2)
            return out.reshape(b, h, n, d)

        def attn_layer(x, Wqkv, qs, ksc, Wo):
            b, n, _ = x.shape
            qkv = x @ Wqkv
            q, k, v = jnp.split(qkv, 3, -1)
            sh = lambda t: t.reshape(b, n, HEADS, DIM_HEAD).transpose(0, 2, 1, 3)
            q, k, v = (sh(q), sh(k), sh(v))
            q = l2norm(q) * qs
            k = l2norm(k) * ksc
            freqs, scale = rotary_tables(n)
            cos, sin = (jnp.cos(freqs), jnp.sin(freqs))
            q = q * cos * scale + rotate_half(q) * sin * scale
            inv = 1.0 / scale
            k = k * cos * inv + rotate_half(k) * sin * inv
            out = local_attention(q, k, v)
            out = out.transpose(0, 2, 1, 3).reshape(b, n, INNER)
            return out @ Wo

        def ffn_layer(x, g, bln, W1, b1, W2, b2):
            mu = x.mean(-1, keepdims=True)
            var = ((x - mu) ** 2).mean(-1, keepdims=True)
            xn = (x - mu) / jnp.sqrt(var + 1e-05) * g + bln
            hg = xn @ W1 + b1
            a, gate = jnp.split(hg, 2, -1)
            return a * jax.nn.gelu(gate, approximate=False) @ W2 + b2
        key = jax.random.key(seed)
        ks = jax.random.split(key, 8)
        B, N = (2, 256)
        init = lambda k, shape: jax.random.normal(k, shape, jnp.float32) * 0.02
        return {'x': jax.random.normal(ks[0], (B, N, DIM), jnp.float32), 'Wqkv': init(ks[1], (DEPTH, DIM, 3 * INNER)), 'q_scale': jnp.ones((DEPTH, DIM_HEAD), jnp.float32), 'k_scale': jnp.ones((DEPTH, DIM_HEAD), jnp.float32), 'Wo': init(ks[2], (DEPTH, INNER, DIM)), 'ln_g': jnp.ones((DEPTH, DIM), jnp.float32), 'ln_b': jnp.zeros((DEPTH, DIM), jnp.float32), 'W1': init(ks[3], (DEPTH, DIM, 2 * DIM_INNER)), 'b1': jnp.zeros((DEPTH, 2 * DIM_INNER), jnp.float32), 'W2': init(ks[4], (DEPTH, DIM_INNER, DIM)), 'b2': jnp.zeros((DEPTH, DIM), jnp.float32)}
    _L0_ffn_in = _L0_ffn_setup()
    _d = {'L0_attn_x': _L0_attn_in['x'], 'L0_attn_Wd_q_w': _L0_attn_in['Wd_q_w'], 'L0_attn_Wd_q_b': _L0_attn_in['Wd_q_b'], 'L0_attn_Wu_q_w': _L0_attn_in['Wu_q_w'], 'L0_attn_Wu_q_b': _L0_attn_in['Wu_q_b'], 'L0_attn_Wq_r_w': _L0_attn_in['Wq_r_w'], 'L0_attn_Wq_r_b': _L0_attn_in['Wq_r_b'], 'L0_attn_Wk_r_w': _L0_attn_in['Wk_r_w'], 'L0_attn_Wk_r_b': _L0_attn_in['Wk_r_b'], 'L0_attn_Wd_kv_w': _L0_attn_in['Wd_kv_w'], 'L0_attn_Wd_kv_b': _L0_attn_in['Wd_kv_b'], 'L0_attn_Wu_k_w': _L0_attn_in['Wu_k_w'], 'L0_attn_Wu_k_b': _L0_attn_in['Wu_k_b'], 'L0_attn_Wu_v_w': _L0_attn_in['Wu_v_w'], 'L0_attn_Wu_v_b': _L0_attn_in['Wu_v_b'], 'L0_attn_Wo_w': _L0_attn_in['Wo_w'], 'L0_attn_Wo_b': _L0_attn_in['Wo_b'], 'L0_ffn_Wqkv': _L0_ffn_in['Wqkv'], 'L0_ffn_q_scale': _L0_ffn_in['q_scale'], 'L0_ffn_k_scale': _L0_ffn_in['k_scale'], 'L0_ffn_Wo': _L0_ffn_in['Wo'], 'L0_ffn_ln_g': _L0_ffn_in['ln_g'], 'L0_ffn_ln_b': _L0_ffn_in['ln_b'], 'L0_ffn_W1': _L0_ffn_in['W1'], 'L0_ffn_b1': _L0_ffn_in['b1'], 'L0_ffn_W2': _L0_ffn_in['W2'], 'L0_ffn_b2': _L0_ffn_in['b2']}
    _x0 = _d['L0_attn_x']
    _d['L0_attn_x'] = jax.random.normal(jax.random.fold_in(jax.random.key(seed), 1), (4, 512, 128), dtype=_x0.dtype)
    del _x0
    return _d

def reference(L0_attn_x, L0_attn_Wd_q_w, L0_attn_Wd_q_b, L0_attn_Wu_q_w, L0_attn_Wu_q_b, L0_attn_Wq_r_w, L0_attn_Wq_r_b, L0_attn_Wk_r_w, L0_attn_Wk_r_b, L0_attn_Wd_kv_w, L0_attn_Wd_kv_b, L0_attn_Wu_k_w, L0_attn_Wu_k_b, L0_attn_Wu_v_w, L0_attn_Wu_v_b, L0_attn_Wo_w, L0_attn_Wo_b, L0_ffn_Wqkv, L0_ffn_q_scale, L0_ffn_k_scale, L0_ffn_Wo, L0_ffn_ln_g, L0_ffn_ln_b, L0_ffn_W1, L0_ffn_b1, L0_ffn_W2, L0_ffn_b2):

    def _L0_attn_ref(x, Wd_q_w, Wd_q_b, Wu_q_w, Wu_q_b, Wq_r_w, Wq_r_b, Wk_r_w, Wk_r_b, Wd_kv_w, Wd_kv_b, Wu_k_w, Wu_k_b, Wu_v_w, Wu_v_b, Wo_w, Wo_b):
        import jax, jax.numpy as jnp
        import numpy as np
        NUM_HEAD = 16
        D_Q = 64
        D_KV = 64
        ROPE_BASE = 10000.0

        def _cos_sin(seq_len, dim):
            pos = jnp.arange(seq_len, dtype=jnp.float32)[:, None]
            ids = jnp.arange(dim // 2, dtype=jnp.float32)
            theta = ROPE_BASE ** (-2.0 * ids) / (dim // 2)
            r = pos * theta[None, :]
            return (jnp.cos(r), jnp.sin(r))

        def _rope(x, cos, sin):
            b, s, d = x.shape
            xv = x.reshape(b, s, d // 2, 2)
            x0, x1 = (xv[..., 0], xv[..., 1])
            out = jnp.stack([x0 * cos - x1 * sin, x1 * cos + x0 * sin], axis=-1)
            return out.reshape(b, s, d)
        b, s, d_model = x.shape
        h = NUM_HEAD
        hd = d_model // h
        scale = jnp.sqrt(jnp.float32(h + D_KV + D_Q))

        def heads(t):
            return t.reshape(b, s, h, hd).transpose(0, 2, 1, 3)
        cos, sin = _cos_sin(s, d_model)
        ct_q = x @ Wd_q_w + Wd_q_b
        qt_c = heads(ct_q @ Wu_q_w + Wu_q_b)
        qt_r = heads(_rope(ct_q @ Wq_r_w + Wq_r_b, cos, sin))
        query = qt_c + qt_r
        ct_kv = x @ Wd_kv_w + Wd_kv_b
        kt_c = heads(ct_kv @ Wu_k_w + Wu_k_b)
        kt_r = heads(_rope(x @ Wk_r_w + Wk_r_b, cos, sin))
        key = kt_c + kt_r
        value = heads(ct_kv @ Wu_v_w + Wu_v_b)
        attn = jnp.einsum('bhqd,bhkd->bhqk', query, key) / scale
        attn = jax.nn.softmax(attn, axis=-1)
        out = jnp.einsum('bhqk,bhkd->bhqd', attn, value)
        out = out.transpose(0, 2, 1, 3).reshape(b, s, d_model)
        return out @ Wo_w + Wo_b

    def _L0_ffn_ref(x, Wqkv, q_scale, k_scale, Wo, ln_g, ln_b, W1, b1, W2, b2):
        import jax, jax.numpy as jnp
        import numpy as np
        DIM = 128
        DEPTH = 6
        HEADS = 16
        DIM_HEAD = 64
        WINDOW = 32
        INNER = HEADS * DIM_HEAD
        DIM_INNER = int(DIM * 4 * 2 / 3)
        QK_SCALE = 8.0

        def shift_tokens(t):
            a, s = jnp.split(t, 2, -1)
            s = jnp.pad(s, ((0, 0), (1, 0), (0, 0)))[:, :-1]
            return jnp.concatenate([a, s], -1)

        def l2norm(t):
            return t / jnp.maximum(jnp.linalg.norm(t, axis=-1, keepdims=True), 1e-12)

        def rotate_half(x):
            x1, x2 = jnp.split(x, 2, -1)
            return jnp.concatenate([-x2, x1], -1)

        def rotary_tables(n):
            half = jnp.arange(0, DIM_HEAD, 2, dtype=jnp.float32)
            inv_freq = 1.0 / 10000.0 ** (half / DIM_HEAD)
            t = jnp.arange(n, dtype=jnp.float32)
            freqs = t[:, None] * inv_freq[None, :]
            freqs = jnp.concatenate([freqs, freqs], -1)
            base_scale = (half + 0.4 * DIM_HEAD) / (1.4 * DIM_HEAD)
            power = (t - n // 2) / (WINDOW // 2)
            scale = base_scale[None, :] ** power[:, None]
            scale = jnp.concatenate([scale, scale], -1)
            return (freqs, scale)

        def local_attention(q, k, v):
            b, h, n, d = q.shape
            w = WINDOW
            nw = n // w
            bq = q.reshape(b, h, nw, w, d)
            bk = k.reshape(b, h, nw, w, d)
            bv = v.reshape(b, h, nw, w, d)

            def look(t):
                p = jnp.pad(t, ((0, 0), (0, 0), (1, 0), (0, 0), (0, 0)))
                return jnp.concatenate([p[:, :, :nw], p[:, :, 1:]], axis=3)
            bk2, bv2 = (look(bk), look(bv))
            seq = jnp.arange(n).reshape(nw, w)
            seq_p = jnp.pad(seq, ((1, 0), (0, 0)), constant_values=-1)
            jt = jnp.concatenate([seq_p[:nw], seq_p[1:]], axis=1)
            it = seq[:, :, None]
            jb = jt[:, None, :]
            mask = (it < jb) | (it > jb + w) | (jb == -1)
            sim = jnp.einsum('bhwie,bhwje->bhwij', bq, bk2) * QK_SCALE
            sim = jnp.where(mask, -jnp.finfo(sim.dtype).max, sim)
            attn = jax.nn.softmax(sim, -1)
            out = jnp.einsum('bhwij,bhwje->bhwie', attn, bv2)
            return out.reshape(b, h, n, d)

        def attn_layer(x, Wqkv, qs, ksc, Wo):
            b, n, _ = x.shape
            qkv = x @ Wqkv
            q, k, v = jnp.split(qkv, 3, -1)
            sh = lambda t: t.reshape(b, n, HEADS, DIM_HEAD).transpose(0, 2, 1, 3)
            q, k, v = (sh(q), sh(k), sh(v))
            q = l2norm(q) * qs
            k = l2norm(k) * ksc
            freqs, scale = rotary_tables(n)
            cos, sin = (jnp.cos(freqs), jnp.sin(freqs))
            q = q * cos * scale + rotate_half(q) * sin * scale
            inv = 1.0 / scale
            k = k * cos * inv + rotate_half(k) * sin * inv
            out = local_attention(q, k, v)
            out = out.transpose(0, 2, 1, 3).reshape(b, n, INNER)
            return out @ Wo

        def ffn_layer(x, g, bln, W1, b1, W2, b2):
            mu = x.mean(-1, keepdims=True)
            var = ((x - mu) ** 2).mean(-1, keepdims=True)
            xn = (x - mu) / jnp.sqrt(var + 1e-05) * g + bln
            hg = xn @ W1 + b1
            a, gate = jnp.split(hg, 2, -1)
            return a * jax.nn.gelu(gate, approximate=False) @ W2 + b2
        for i in range(DEPTH):
            x = attn_layer(shift_tokens(x), Wqkv[i], q_scale[i], k_scale[i], Wo[i]) + x
            x = ffn_layer(shift_tokens(x), ln_g[i], ln_b[i], W1[i], b1[i], W2[i], b2[i]) + x
        return x
    x = L0_attn_x
    x = _layernorm(x + _L0_attn_ref(x, L0_attn_Wd_q_w, L0_attn_Wd_q_b, L0_attn_Wu_q_w, L0_attn_Wu_q_b, L0_attn_Wq_r_w, L0_attn_Wq_r_b, L0_attn_Wk_r_w, L0_attn_Wk_r_b, L0_attn_Wd_kv_w, L0_attn_Wd_kv_b, L0_attn_Wu_k_w, L0_attn_Wu_k_b, L0_attn_Wu_v_w, L0_attn_Wu_v_b, L0_attn_Wo_w, L0_attn_Wo_b), axis=-1)
    x = _layernorm(x + _L0_ffn_ref(x, L0_ffn_Wqkv, L0_ffn_q_scale, L0_ffn_k_scale, L0_ffn_Wo, L0_ffn_ln_g, L0_ffn_ln_b, L0_ffn_W1, L0_ffn_b1, L0_ffn_W2, L0_ffn_b2), axis=-1)
    return x

_drawn_inputs = setup_inputs


def setup_inputs(seed=0):
    import zlib

    import numpy as np

    out = dict(_drawn_inputs(seed))
    spreads = {'L0_attn_Wd_q_b': (0.0, 0.8),
     'L0_attn_Wu_q_b': (0.0, 0.8),
     'L0_attn_Wq_r_b': (0.0, 0.8),
     'L0_attn_Wk_r_b': (0.0, 0.8),
     'L0_attn_Wd_kv_b': (0.0, 0.8),
     'L0_attn_Wu_k_b': (0.0, 0.8),
     'L0_attn_Wu_v_b': (0.0, 0.363),
     'L0_attn_Wo_b': (0.0, 0.1),
     'L0_ffn_q_scale': (1.0, 0.6),
     'L0_ffn_k_scale': (1.0, 0.6),
     'L0_ffn_ln_g': (1.0, 0.6),
     'L0_ffn_ln_b': (0.0, 0.8),
     'L0_ffn_b1': (0.0, 0.8),
     'L0_ffn_b2': (0.0, 0.1)}
    factors = {'L0_attn_Wd_q_w': 8.0,
     'L0_attn_Wu_q_w': 8.0,
     'L0_attn_Wq_r_w': 8.0,
     'L0_attn_Wk_r_w': 8.0,
     'L0_attn_Wd_kv_w': 8.0,
     'L0_attn_Wu_k_w': 8.0,
     'L0_attn_Wu_v_w': 8.0,
     'L0_ffn_W1': 3.675,
     'L0_ffn_W2': 3.615}
    for name, (base, spread) in spreads.items():
        noise = np.random.default_rng([zlib.crc32(name.encode()), seed]).standard_normal(out[name].shape)
        drawn = base * np.exp(spread * noise) if base else spread * noise
        out[name] = jnp.asarray(drawn.astype(out[name].dtype))
    for name, factor in factors.items():
        out[name] = (out[name] * factor).astype(out[name].dtype)
    return out
```

```python
from contextlib import ExitStack

import numpy as np
import concourse.bass as bass
from concourse import mybir

F32 = mybir.dt.float32
BF16 = mybir.dt.bfloat16
ACT = mybir.ActivationFunctionType
ALU = mybir.AluOpType
AX = mybir.AxisListType

B, S, D = 4, 512, 128
NT = S // 128
H = 16
HD = D // H
LAT = 64
SCORE_SCALE = 1.0 / float(np.sqrt(np.float32(H + LAT + LAT)))
DEPTH = 6
DH = 64
HP = H // 2
W = 32
QK_SCALE = 8.0
FI = int(D * 4 * 2 / 3)
FC = [min(128, FI - c) for c in range(0, FI, 128)]
EPS = 1e-5
NIT = DEPTH * B
TERMS = 9
ROWS = TERMS * HD


def dense_attention(nc, a, keep):
    q_parts = nc.dram_tensor("q_parts", [3, 128, S], BF16, kind="Internal").ap()
    k_parts = nc.dram_tensor("k_parts", [3, 128, S], BF16, kind="Internal").ap()
    m_parts = nc.dram_tensor("m_parts", [3, H * NT, 128], BF16, kind="Internal").ap()
    with ExitStack() as c:
        def sb(name, shape, dt=F32):
            return c.enter_context(nc.sbuf_tensor(name, shape, dt))

        def sem(name):
            return c.enter_context(nc.semaphore(name))

        wA = sb("wA", [128, 3, 128])
        wU = sb("wU", [128, 3, 128])
        wO = sb("wO", [128, 128])
        bcol = sb("bcol", [128, 7])
        brow = sb("brow", [128, 2, 128])
        rope = sb("rope", [128, 2, S])
        x_b = sb("x_b", [128, NT, 128])
        xT = sb("xT", [128, S])
        lat = sb("lat", [128, S])
        t_cos = sb("t_cos", [128, S])
        t_sin = sb("t_sin", [128, S])
        q_f = sb("q_f", [128, S])
        rest = sb("rest", [128, S])
        part = sb("part", [128, 2, 3, S], BF16)
        Q9 = sb("Q9", [ROWS + 3, H, S], BF16)
        K9 = sb("K9", [ROWS + 3, H, S], BF16)
        V = sb("V", [128, NT, H, 32])
        negmax = sb("negmax", [128, H, NT])
        nm_rest = sb("nm_rest", [4 * NT, 128])
        nm_part = sb("nm_part", [4 * NT, 3, 128], BF16)
        P = sb("P", [128, 2, 4, NT, S])
        pv_sb = sb("pv_sb", [128, S])
        rden = sb("rden", [128, NT, 4])
        o_t = sb("o_t", [128, NT, H, HD])
        oT = sb("oT_a", [128, S])
        y = sb("y", [128, NT, 128])
        stats = sb("stats_a", [128, NT, 6])
        mv = sb("mv_a", [128, NT, 2])
        rstd = sb("rstd_a", [128, NT])
        ps_d = [c.enter_context(nc.psum_tensor(f"ps_d{i}", [128, S], F32)) for i in range(2)]
        ps_a = [c.enter_context(nc.psum_tensor(f"ps_a{i}", [128, 2, S], F32)) for i in range(2)]
        ps_pv = c.enter_context(nc.psum_tensor("ps_pv", [128, S], F32))
        ps_m = c.enter_context(nc.psum_tensor("ps_m", [128, S], F32))

        s_w = sem("a_weights")
        s_x = sem("a_x_loaded")
        s_const = sem("a_const")
        d_full, d_free = sem("ps_d_full"), sem("ps_d_free")
        a_full, a_free = sem("ps_a_full"), sem("ps_a_free")
        pv_full, pv_free = sem("ps_pv_full"), sem("ps_pv_free")
        m_full, m_free = sem("ps_m_full"), sem("ps_m_free")
        s_dve = sem("a_dve_chain")
        s_part = sem("a_parts_split")
        s_scr = sem("a_parts_in_dram")
        s_stack = sem("a_stacked")
        s_nmp = sem("a_negmax_split")
        s_nscr = sem("a_negmax_in_dram")
        s_nrow = [sem(f"a_negmax_rows{g}") for g in range(H // 4)]
        s_stats, s_aggr, s_mv = sem("a_stats_done"), sem("a_aggr_begun"), sem("a_mv_done")
        s_var = sem("a_var_done")
        s_rstd = sem("a_rstd_done")
        s_y = sem("a_y_normalised")

        ND = 7 + H * NT + 1
        NA = 2 + 2 * H + 2
        NM = 8
        G = H // 4
        block = c.enter_context(nc.Block())

        steps = [(0, None, None), (1, None, None), (2, 0, None), (3, 1, 0), (None, 2, 1), (None, 3, 2), (None, None, 3)]

        @block.sync
        def _(sp):
            for dst, src in ((wA, a["wA"]), (wU, a["wU"]), (wO, a["wO"]), (bcol, a["bcol"]), (rope, a["rope"]),
                             (keep.ident, a["ident"])):
                sp.dma_start(dst[:], src).then_inc(s_w, 16)
            sp.dma_start(brow[:], a["brow"].rearrange("(o r) n -> o r n", o=1).broadcast_to([128, 2, 128])).then_inc(s_w, 16)
            with sp.Fori(0, B) as b:
                sp.wait_ge(d_free, ND * b + 2)
                sp.dma_start(x_b[:], a["x"][bass.ds(b, 1), :, :].rearrange("o (t p) d -> p (o t) d", p=128)).then_inc(s_x, 16)
                for k, (scr, dst) in enumerate(((q_parts, Q9), (k_parts, K9))):
                    sp.wait_ge(s_part, 2 * b + k + 1)
                    sp.dma_start(scr.rearrange("a p s -> p a s"), part[:, k]).then_inc(s_scr, 16)
                    sp.wait_ge(s_scr, 32 * b + 16 * (k + 1))
                    if k == 0:
                        for pa in range(3):
                            src = q_parts[pa].rearrange("(o d h) s -> o d (h s)", o=1, d=HD).broadcast_to([3, HD, H * S])
                            sp.dma_start(Q9[24 * pa:24 * pa + 24, :, :], src).then_inc(s_stack, 16)
                    else:
                        src = k_parts.rearrange("b (d h) s -> (b d) (h s)", d=HD)
                        for pa in range(3):
                            sp.dma_start(K9[24 * pa:24 * pa + 24, :, :], src).then_inc(s_stack, 16)
                for g in range(G):
                    sp.wait_ge(s_nmp, 4 * b + g + 1)
                    sp.dma_start(m_parts[:, 16 * g:16 * g + 16, :].rearrange("a r q -> r a q"), nm_part[:]).then_inc(s_nscr, 16)
                    sp.wait_ge(s_nscr, 64 * b + 16 * (g + 1))
                    sp.dma_start(Q9[ROWS:ROWS + 3, 4 * g:4 * g + 4, :],
                                 m_parts[:, 16 * g:16 * g + 16, :].rearrange("a (h t) q -> a h (t q)", h=4)).then_inc(s_nrow[g], 16)

        @block.gpsimd
        def _(pool):
            nc.gpsimd.memset(V[:], 0.0).then_inc(s_const, 1)
            nc.gpsimd.memset(K9[:], 1.0).then_inc(s_const, 1)
            nc.gpsimd.memset(keep.half[:], -0.5).then_inc(s_const, 1)
            pool.wait_ge(s_const, 3)
            nc.gpsimd.memset(V[:, :, :, HD:HD + 1], 1.0).then_inc(s_const, 1)
            with pool.Fori(0, B) as b:
                pool.wait_ge(s_var, b + 1)
                nc.gpsimd.tensor_tensor(rstd[:], mv[:, :, 1], keep.half[:, 0:NT], ALU.pow).then_inc(s_rstd, 1)

        @block.tensor
        def _(pe):
            pe.wait_ge(s_w, 16 * 7)
            pe.wait_ge(s_const, 4)
            with pe.Fori(0, B) as b:
                nd, na, nm = [0], [0], [0]

                def bank_d():
                    k = nd[0]
                    nd[0] += 1
                    pe.wait_ge(d_free, ND * b + k + 1)
                    return ps_d[k % 2]

                def bank_a():
                    k = na[0]
                    na[0] += 1
                    pe.wait_ge(a_free, NA * b + k + 1)
                    return ps_a[k % 2]

                def bank_m():
                    k = nm[0]
                    nm[0] += 1
                    pe.wait_ge(m_free, NM * b + k + 1)
                    return ps_m

                ps = bank_a()
                pe.wait_ge(s_x, 16 * (b + 1))
                for t in range(NT):
                    last = nc.tensor.transpose(ps[:, 0, 128 * t:128 * t + 128], x_b[:, t, :], keep.ident[:])
                last.then_inc(a_full, 1)
                ps = bank_a()
                pe.wait_ge(a_free, NA * b + 3)
                nc.tensor.matmul(ps[:, 0, :], wA[:, 0, :], xT[:], start=True, stop=True).then_inc(a_full, 1)
                pe.wait_ge(a_free, NA * b + 4)
                ql, kl = slice(0, LAT), slice(LAT, 2 * LAT)
                for lhsT, rhs in ((wU[ql, 1, :], lat[ql, :]), (wU[ql, 2, :], lat[ql, :]), (wU[ql, 0, :], lat[ql, :]),
                                  (wA[:, 1, :], xT[:]), (wA[:, 2, :], xT[:]), (wU[kl, 0, :], lat[kl, :])):
                    nc.tensor.matmul(bank_d()[:], lhsT, rhs, start=True, stop=True).then_inc(d_full, 1)
                ps = bank_d()
                for t in range(NT):
                    last = nc.tensor.matmul(ps[:, 128 * t:128 * t + 128], lat[kl, 128 * t:128 * t + 128], wU[kl, 1, :],
                                            start=True, stop=True)
                last.then_inc(d_full, 1)
                pe.wait_ge(s_stack, 96 * (b + 1))
                def max_scores(h):
                    for t in range(NT):
                        nc.tensor.matmul(bank_d()[:], Q9[0:ROWS, h, 128 * t:128 * t + 128], K9[0:ROWS, h, :],
                                         start=True, stop=True).then_inc(d_full, 1)

                def exp_scores(h):
                    for u in range(2):
                        ps = bank_a()
                        for t in range(2):
                            k0 = 128 * (2 * u + t)
                            last = nc.tensor.matmul(ps[:, t, :], K9[:, h, k0:k0 + 128], Q9[:, h, :], start=True, stop=True)
                        last.then_inc(a_full, 1)

                for gm, ge, gv in steps:
                    if ge is not None:
                        pe.wait_ge(s_nrow[ge], 16 * (b + 1))
                    for i in range(4):
                        if gm is not None:
                            max_scores(4 * gm + i)
                        if ge is not None:
                            exp_scores(4 * ge + i)
                    if gm is not None:
                        ps = bank_m()
                        pe.wait_ge(d_free, ND * b + 2 + 7 + 4 * NT * (gm + 1))
                        nc.tensor.transpose(ps[0:4 * NT, 0:128], negmax[:, 4 * gm:4 * gm + 4, :].rearrange("p h t -> p (h t)"),
                                            keep.ident[:]).then_inc(m_full, 1)
                    if gv is not None:
                        pe.wait_ge(pv_free, 4 * b + gv + 1)
                        pe.wait_ge(a_free, NA * b + 2 + 2 + 8 * (gv + 1))
                        for t in range(NT):
                            for h in range(4):
                                last = nc.tensor.matmul(ps_pv[32 * h:32 * h + 32, :], V[:, t, 4 * gv + h, :], P[:, gv % 2, h, t, :],
                                                        start=t == 0, stop=t == NT - 1, skip_group_check=True)
                        last.then_inc(pv_full, 1)
                        ps = bank_m()
                        pe.wait_ge(pv_free, 4 * b + gv + 2)
                        for t in range(NT):
                            last = nc.tensor.transpose(ps[:, 128 * t:128 * t + 128], pv_sb[:, 128 * t:128 * t + 128], keep.ident[:])
                        last.then_inc(m_full, 1)
                ps = bank_a()
                pe.wait_ge(m_free, NM * (b + 1) + 1)
                for t in range(NT):
                    last = nc.tensor.transpose(ps[:, 0, 128 * t:128 * t + 128], o_t[:, t].rearrange("p h d -> p (h d)"), keep.ident[:])
                last.then_inc(a_full, 1)
                ps = bank_d()
                pe.wait_ge(a_free, NA * (b + 1) + 1)
                for t in range(NT):
                    last = nc.tensor.matmul(ps[:, 128 * t:128 * t + 128], oT[:, 128 * t:128 * t + 128], wO[:], start=True, stop=True)
                last.then_inc(d_full, 1)
                ps = bank_a()
                pe.wait_ge(s_y, NT * (b + 1))
                for t in range(NT):
                    last = nc.tensor.transpose(ps[:, 0, 128 * t:128 * t + 128], y[:, t, :], keep.ident[:])
                last.then_inc(a_full, 1)
                assert (nd[0], na[0], nm[0]) == (ND, NA, NM)

        @block.scalar
        def _(act):
            act.preload_act_table(ACT.Exp)
            act.sem_inc(a_free, 2)
            act.sem_inc(pv_free, 1)
            act.wait_ge(s_w, 16 * 7)
            with act.Fori(0, B) as b:
                na = [0]

                def full():
                    k = na[0]
                    na[0] += 1
                    act.wait_ge(a_full, NA * b + k + 1)
                    return ps_a[k % 2]

                ps = full()
                nc.scalar.copy(xT[:], ps[:, 0, :]).then_inc(a_free, 1)
                ps = full()
                nc.scalar.activation(lat[:], ps[:, 0, :], ACT.Identity, bias=bcol[:, 0:1]).then_inc(a_free, 1)
                for gm, ge, gv in steps:
                    if ge is not None:
                        for h in range(4):
                            for u in range(2):
                                ps = full()
                                nc.scalar.activation(P[:, ge % 2, h, 2 * u:2 * u + 2, :], ps[:], ACT.Exp,
                                                     scale=SCORE_SCALE).then_inc(a_free, 1)
                    if gv is not None:
                        act.wait_ge(pv_full, 4 * b + gv + 1)
                        nc.scalar.copy(pv_sb[:], ps_pv[:]).then_inc(pv_free, 1)
                ps = full()
                nc.scalar.copy(oT[:], ps[:, 0, :]).then_inc(a_free, 1)
                ps = full()
                nc.scalar.copy(keep.xF[:, bass.ds(b * S, S)], ps[:, 0, :]).then_inc(a_free, 1)

        @block.vector
        def _(dve):
            dve.sem_inc(d_free, 2)
            dve.sem_inc(m_free, 1)
            dve.wait_ge(s_w, 16 * 7)
            dve.wait_ge(s_const, 4)
            CH = 2 * 4 + G * 3 + 1 + 1
            with dve.Fori(0, B) as b:
                nd, nm, ch = [0], [0], [0]

                def full():
                    k = nd[0]
                    nd[0] += 1
                    dve.wait_ge(d_full, ND * b + k + 1)
                    return ps_d[k % 2]

                def full_m():
                    k = nm[0]
                    nm[0] += 1
                    dve.wait_ge(m_full, NM * b + k + 1)
                    return ps_m

                def then(ins):
                    ch[0] += 1
                    ins.then_inc(s_dve, 1)
                    dve.wait_ge(s_dve, CH * b + ch[0])

                for k in range(2):
                    bias = 1 + 3 * k
                    nc.vector.scalar_tensor_tensor(t_cos[:], full()[:], bcol[:, bias + 1:bias + 2], rope[:, 0, :], ALU.add, ALU.mult).then_inc(d_free, 1)
                    nc.vector.scalar_tensor_tensor(t_sin[:], full()[:], bcol[:, bias + 2:bias + 3], rope[:, 1, :], ALU.add, ALU.mult).then_inc(d_free, 1)
                    dve.wait_ge(d_free, ND * b + 2 + 3 * k + 2)
                    then(nc.vector.tensor_tensor(t_cos[:], t_cos[:], t_sin[:], ALU.add))
                    nc.vector.scalar_tensor_tensor(q_f[:], full()[:], bcol[:, bias:bias + 1], t_cos[:], ALU.add, ALU.add).then_inc(d_free, 1)
                    dve.wait_ge(d_free, ND * b + 2 + 3 * k + 3)
                    then(nc.vector.tensor_copy(part[:, k, 0, :], q_f[:]))
                    then(nc.vector.tensor_tensor(rest[:], q_f[:], part[:, k, 0, :], ALU.subtract))
                    then(nc.vector.tensor_copy(part[:, k, 1, :], rest[:]))
                    nc.vector.tensor_tensor(part[:, k, 2, :], rest[:], part[:, k, 1, :], ALU.subtract).then_inc(s_part, 1)
                ps = full()
                nc.vector.tensor_tensor(V[:, :, :, 0:HD], ps[:].rearrange("p (t h d) -> p t h d", t=NT, h=H),
                                        brow[:, 0:1, :].rearrange("p o (h d) -> p o h d", h=H).broadcast_to([128, NT, H, HD]),
                                        ALU.add).then_inc(d_free, 1)
                for gm, ge, gv in steps:
                    if gm is not None:
                        for h in range(4 * gm, 4 * gm + 4):
                            for t in range(NT):
                                nc.vector.tensor_reduce(negmax[:, h, t:t + 1], full()[:], AX.X, ALU.max, negate=True).then_inc(d_free, 1)
                        ps = full_m()
                        if gm:
                            dve.wait_ge(s_nscr, 64 * b + 16 * gm)
                        then(nc.vector.tensor_copy(nm_part[:, 0, :], ps[0:4 * NT, 0:128]))
                        nc.vector.tensor_tensor(nm_rest[:], ps[0:4 * NT, 0:128], nm_part[:, 0, :], ALU.subtract).then_inc(m_free, 1)
                        dve.wait_ge(m_free, NM * b + nm[0] + 1)
                        then(nc.vector.tensor_copy(nm_part[:, 1, :], nm_rest[:]))
                        nc.vector.tensor_tensor(nm_part[:, 2, :], nm_rest[:], nm_part[:, 1, :], ALU.subtract).then_inc(s_nmp, 1)
                    if gv is not None:
                        ps = full_m()[:].rearrange("p (t h d) -> p t h d", t=NT, h=4)
                        then(nc.vector.reciprocal(rden[:], ps[:, :, :, HD]))
                        nc.vector.tensor_tensor(o_t[:, :, 4 * gv:4 * gv + 4, :], ps[:, :, :, 0:HD],
                                                rden[:].rearrange("p t (h o) -> p t h o", o=1).broadcast_to([128, NT, 4, HD]),
                                                ALU.mult).then_inc(m_free, 1)
                ps = full()
                nc.vector.tensor_tensor(y[:], ps[:].rearrange("p (t n) -> p t n", t=NT), x_b[:], ALU.add).then_inc(d_free, 1)
                dve.wait_ge(d_free, ND * (b + 1) + 2)
                then(nc.vector.tensor_tensor(y[:], y[:], brow[:, 1:2, :].broadcast_to([128, NT, 128]), ALU.add))
                for t in range(NT):
                    nc.vector.bn_stats(stats[:, t, :], y[:, t, :]).then_inc(s_stats, 1)
                dve.wait_ge(s_stats, NT * (b + 1))
                dve.sem_inc(s_aggr, 1)
                for t in range(NT):
                    nc.vector.bn_aggr(mv[:, t, :], stats[:, t, :]).then_inc(s_mv, 1)
                dve.wait_ge(s_mv, NT * (b + 1))
                nc.vector.tensor_scalar(mv[:, :, 1], mv[:, :, 1], EPS, None, ALU.add).then_inc(s_var, 1)
                dve.wait_ge(s_rstd, b + 1)
                for t in range(NT):
                    nc.vector.tensor_scalar(y[:, t, :], y[:, t, :], mv[:, t, 0:1], rstd[:, t:t + 1],
                                            ALU.subtract, ALU.mult).then_inc(s_y, 1)
                dve.wait_ge(s_y, NT * (b + 1))
                then(nc.vector.tensor_copy(keep.x1[:, bass.ds(b * NT, NT), :], y[:]))
                assert ch[0] == CH, ch


class Uses:

    def __init__(self, per_turn):
        self.per_turn, self.n, self.in_loop = per_turn, 0, 0

    def enter_loop(self, turn):
        self.in_loop, self.entered = turn * self.per_turn, self.n

    def leave_loop(self, turns):
        assert self.n == self.entered + self.per_turn
        self.n, self.in_loop = self.entered + turns * self.per_turn, 0

    def next(self):
        n = self.n
        self.n += 1
        return self.in_loop + n, n


def local_layers(nc, a, keep):
    with ExitStack() as c:
        def sb(name, shape, dt=F32):
            return c.enter_context(nc.sbuf_tensor(name, shape, dt))

        def sem(name):
            return c.enter_context(nc.semaphore(name))

        wqk = sb("wqk", [128, 2 * H * DH])
        wv = sb("wv", [128, 2, HP * DH])
        wo = sb("wo", [128, HP, D])
        w1 = sb("w1", [128, 2 * FI])
        w2 = sb("w2", [128, len(FC), D])
        cols = sb("cols", [128, 9])
        scales = sb("scales", [128, 4 * DH])
        tab = sb("tab", [128, NT, 4 * DH])
        mask_f = sb("mask_f", [128, 2, 2 * W])
        mask = sb("mask_bf", [128, 2, 8, 2 * W], BF16)
        ident_b = sb("ident_b", [128, 128], BF16)

        xs = sb("xs", [128, W + S])
        qk = sb("qk", [128, 2 * H, DH])
        sq = sb("sq", [128, 2 * H, DH])
        rcos = sb("rcos", [128, 2 * H, DH])
        rot = sb("rot", [128, 2 * H, DH])
        rsin = sb("rsin", [128, 2 * H, DH])
        ss = sb("ss", [128, 2 * H])
        rn = sb("rn", [128, 2 * H])
        st = sb("scaled_tab", [128, 4 * DH])
        qT = sb("qT", [128, HP, S])
        kT = sb("kT", [128, HP, W + S])
        V = sb("Vw", [128, S // W, HP, DH + 1])
        P = sb("Pl", [128, 2, 8, 2 * W])
        ss_max = sb("ss_max", [128, 8])
        PT = sb("PT", [128, 2, 4, 128])
        rden = sb("rden_l", [128, 2, 4])
        o = sb("o_l", [128, 2, 4, 2, DH])
        oT = sb("oT", [128, HP, S])
        xs2 = sb("xs2", [128, S])
        stats = sb("stats", [128, NT, 6])
        mv = sb("mv", [128, NT, 2])
        rstd = sb("rstd", [128, NT])
        xn = sb("xn", [128, NT, D])
        xnT = sb("xnT", [128, S])
        gate = sb("gate", [128, len(FC), S])
        hid = sb("hid", [128, len(FC), S])

        ps_p = [c.enter_context(nc.psum_tensor(f"ps_p{i}", [128, S], F32)) for i in range(2)]
        ps_t = [c.enter_context(nc.psum_tensor(f"ps_t{i}", [128, S], F32)) for i in range(2)]
        ps_s = c.enter_context(nc.psum_tensor("ps_s", [128, 8, 2 * W], F32))
        ps_o = c.enter_context(nc.psum_tensor("ps_o", [128, 2, S], F32))
        ps_f = c.enter_context(nc.psum_tensor("ps_f", [128, S], F32))

        s_c = sem("b_const_loaded")
        s_init = sem("b_init")
        s_initv = sem("b_init_vector")
        ld = {n: sem("ld_" + n) for n in ("wqk", "scales", "wv", "wo", "cols", "w1", "w2")}
        ready = {n: sem("ready_" + n) for n in ld}
        tab_made = sem("tab_made")
        p_full, p_free = sem("ps_p_full"), sem("ps_p_free")
        t_full, t_free = sem("ps_t_full"), sem("ps_t_free")
        f_full, f_free = sem("ps_f_full"), sem("ps_f_free")
        s_full, max_done, sub_done, exp_done = sem("scores_done"), sem("max_done"), sem("sub_done"), sem("exp_done")
        pv_done, rden_done, o_done = sem("pv_done"), sem("rden_done"), sem("o_done")
        xs_done = sem("xs_done")
        sq_done, ss_done, rm_done, rn_done = (sem(n) for n in ("sq_done", "ss_done", "rm_done", "rn_done"))
        sum_done, cos_done, sin_done, rope_done = sem("sum_done"), sem("cos_done"), sem("sin_done"), sem("rope_done")
        xs2_done = sem("xs2_done")
        values_begun, aggr_begun = sem("values_begun"), sem("aggr_begun")
        st_done, mv_done, var_done, rstd_done = sem("stats_done"), sem("mv_done"), sem("var_done"), sem("rstd_done")

        PROJ, TR, FF = 8 * NT, 16 + 8 + 8 + 1 + 3, 6
        block = c.enter_context(nc.Block())

        def turns(engine, body, counters):
            body(0, True, False)
            with engine.Fori(1, NIT - 1) as it:
                for u in counters:
                    u.enter_loop(it - 1)
                body(it, False, False)
            for u in counters:
                u.leave_loop(NIT - 2)
            body(NIT - 1, False, True)

        def ahead(it, t):
            return it + t // NT, t % NT

        @block.sync
        def _(sp):
            sp.dma_start(tab[:], a["tab"]).then_inc(s_c, 16)
            sp.dma_start(mask_f[:], a["mask"]).then_inc(s_c, 16)

            def src(n, layer):
                if n == "scales":
                    return a[n][bass.ds(layer, 1)].rearrange("o k d -> o (k d)").broadcast_to([128, 4 * DH])
                names = "o p " + " ".join("xyz"[:len(a[n].shape) - 2])
                return a[n][bass.ds(layer, 1)].rearrange(names + " -> p (o " + names[4:] + ")")

            def flat(x):
                return x[:] if len(x.shape) == 2 else x[:].rearrange("p a b -> p (a b)")

            dst = {"wqk": wqk, "scales": scales, "wv": wv, "wo": wo, "cols": cols, "w1": w1, "w2": w2}
            used = {"wqk": (p_full, PROJ * B, -4), "scales": (tab_made, NT * B, 0), "wv": (p_full, PROJ * B, 0),
                    "wo": (f_full, FF * B, 1 - FF), "cols": (f_free, FF * B, 1), "w1": (f_full, FF * B, 0), "w2": (f_full, FF * B, 0)}

            def load(layer, first):
                for group in (("wqk", "scales", "wv"), ("wo",), ("cols", "w1", "w2")):
                    for n in group:
                        if not first:
                            sem_used, per_layer, more = used[n]
                            sp.wait_ge(sem_used, layer * per_layer + more)
                        sp.dma_start(flat(dst[n]), src(n, layer)).then_inc(ld[n], 16)
                    for n in group:
                        sp.wait_ge(ld[n], 16 * (layer + 1))
                        sp.sem_inc(ready[n], B)

            load(0, True)
            with sp.Fori(1, DEPTH) as layer:
                load(layer, False)

        @block.gpsimd
        def _(pool):
            nc.gpsimd.memset(xs[:], 0.0).then_inc(s_init, 1)
            nc.gpsimd.memset(kT[:], 0.0).then_inc(s_init, 1)
            nc.gpsimd.memset(V[:], 1.0).then_inc(s_init, 1)
            pool.wait_ge(s_init, 3)
            pool.wait_ge(s_c, 32)

            def tables(it, t):
                it2, t2 = ahead(it, t)
                tiles = NT * it + t
                if t2 == 0:
                    pool.wait_ge(ready["scales"], it2 + 1)
                if not (isinstance(tiles, int) and tiles == 0):
                    pool.wait_ge(cos_done, tiles)
                    pool.wait_ge(sin_done, 2 * tiles)
                nc.gpsimd.tensor_tensor(st[:], tab[:, t2, :], scales[:], ALU.mult).then_inc(tab_made, 1)

            def sin_part(it, t):
                tiles = NT * it + t
                pool.wait_ge(p_free, 2 + 8 * tiles + 4)
                pool.wait_ge(tab_made, tiles + 1)
                if not (isinstance(tiles, int) and tiles == 0):
                    pool.wait_ge(sum_done, tiles)
                n4 = qk[:].rearrange("p (k h) (e d) -> p k h e d", k=2, e=2)
                r4 = rsin[:].rearrange("p (k h) (e d) -> p k h e d", k=2, e=2)
                sin = st[:, 2 * DH:4 * DH].rearrange("p (k o e d) -> p k o e d", k=2, o=1, e=2)
                for e in range(2):
                    nc.gpsimd.tensor_tensor(r4[:, :, :, e, :], n4[:, :, :, 1 - e, :],
                                            sin[:, :, :, e, :].broadcast_to([128, 2, H, DH // 2]), ALU.mult).then_inc(sin_done, 1)

            def inverse_norms(it, t):
                tiles = NT * it + t
                pool.wait_ge(rm_done, tiles + 1)
                nc.gpsimd.tensor_tensor(rn[:], ss[:], keep.half[:, 0:2 * H], ALU.pow).then_inc(rn_done, 1)

            def rstd_of(it):
                pool.wait_ge(var_done, it + 1)
                nc.gpsimd.tensor_tensor(rstd[:], mv[:, :, 1], keep.half[:, 0:NT], ALU.pow).then_inc(rstd_done, 1)

            nc.gpsimd.memset(xs2[:], 0.0).then_inc(s_init, 1)
            pool.wait_ge(s_init, 4)
            for t in range(2):
                tables(0, t)
                sin_part(0, t)
                inverse_norms(0, t)

            def body(it, first, last):
                for s in range(8):
                    t, hh = s // 2, s % 2
                    if hh == 0 and not (last and t + 2 >= NT):
                        tables(it, t + 2)
                        sin_part(it, t + 2)
                        inverse_norms(it, t + 2)
                    if s == 3 and not first:
                        rstd_of(it - 1)

            turns(pool, body, [])
            rstd_of(NIT - 1)

        @block.tensor
        def _(pe):
            up, ut, uf = Uses(PROJ), Uses(TR), Uses(FF)
            ident = keep.ident
            pe.wait_ge(s_init, 4)
            pe.wait_ge(s_initv, 3)

            def bank_p():
                n, bank = up.next()
                pe.wait_ge(p_free, n + 1)
                return ps_p[bank % 2]

            copied = {}

            def bank_t(what=None):
                n, bank = ut.next()
                pe.wait_ge(t_free, n + 1)
                copied[what] = n + 3
                return ps_t[bank % 2]

            def bank_f():
                n, _ = uf.next()
                pe.wait_ge(f_free, n + 1)
                return ps_f

            def project_qk(it, t, after=lambda j: None):
                it2, t2 = ahead(it, t)
                if t2 == 0:
                    pe.wait_ge(ready["wqk"], it2 + 1)
                pe.wait_ge(xs_done, 2 * (NT * it + t + 1))
                for j in range(4):
                    nc.tensor.matmul(bank_p()[:], xs[:, W + 128 * t2:W + 128 * t2 + 128], wqk[:, S * j:S * j + S],
                                     start=True, stop=True).then_inc(p_full, 1)
                    after(j)

            def project_v(it, t, windows):
                it2, t2 = ahead(it, t)
                if t2 == 0:
                    pe.wait_ge(ready["wv"], it2 + 1)
                for w in windows:
                    ps = bank_p()
                    for e in range(2):
                        last = nc.tensor.matmul(ps[64 * e:64 * e + 64, :], xs[:, 128 * t2 + W * w:128 * t2 + W * w + 2 * W],
                                                wv[:, e, :], start=True, stop=True, skip_group_check=True)
                    last.then_inc(p_full, 1)

            def transpose_qk(it, t, parts):
                pe.wait_ge(rope_done, NT * it + t + 1)
                flat = rot[:].rearrange("p h d -> p (h d)")
                for j in parts:
                    ps = bank_t()
                    for i in range(4):
                        last = nc.tensor.transpose(ps[:, 128 * i:128 * i + 128], flat[:, S * j + 128 * i:S * j + 128 * i + 128], ident[:])
                    last.then_inc(t_full, 1)

            def scores(it, s):
                t, hh = s // 2, s % 2
                n = 8 * it + s
                if not (isinstance(n, int) and n == 0):
                    pe.wait_ge(sub_done, n)
                nc.tensor.matmul(ps_s[:], ident_b[:], mask[:, 0 if t == 0 else 1, :, :], start=True, stop=False, skip_group_check=True)
                rows = slice(64 * hh, 64 * hh + 64)
                for j in range(8):
                    for w in range(4):
                        q0 = 128 * t + W * w
                        last = nc.tensor.matmul(ps_s[W * w:W * w + W, j, :], qT[rows, j, q0:q0 + W],
                                                kT[rows, j, q0:q0 + 2 * W], start=False, stop=True, skip_group_check=True)
                last.then_inc(s_full, 1)

            def transpose_p(n, bank):
                pe.wait_ge(exp_done, n + 1)
                ps = bank_t("PT")
                for j in range(4):
                    last = nc.tensor.transpose(ps[:, 128 * j:128 * j + 128], P[:, bank, 2 * j:2 * j + 2, :].rearrange("p e k -> p (e k)"), ident[:])
                last.then_inc(t_full, 1)

            def values(it, s):
                t, hh = s // 2, s % 2
                n = 8 * it + s
                pe.wait_ge(t_free, copied["PT"])
                pe.wait_ge(p_free, 2 + 8 * (NT * it + t + 1))
                if not (isinstance(n, int) and n == 0):
                    pe.wait_ge(o_done, n)
                pe.sem_inc(values_begun, 1)
                for j in range(4):
                    for e in range(2):
                        for w in range(4):
                            rows = slice(64 * e, 64 * e + 64)
                            last = nc.tensor.matmul(ps_o[W * w:W * w + W, e, (DH + 1) * j:(DH + 1) * (j + 1)],
                                                    PT[rows, s % 2, j, W * w:W * w + W], V[rows, 4 * t + w, 4 * hh + j, :],
                                                    start=True, stop=True, skip_group_check=True)
                last.then_inc(pv_done, 1)

            def transpose_o(n, bank):
                pe.wait_ge(o_done, n + 1)
                ps = bank_t("oT")
                for j in range(4):
                    last = nc.tensor.transpose(ps[:, 128 * j:128 * j + 128], o[:, bank, j, :, :].rearrange("p e d -> p (e d)"), ident[:])
                last.then_inc(t_full, 1)

            def output_projection(it):
                ps = bank_f()
                pe.wait_ge(ready["wo"], it + 1)
                pe.wait_ge(t_free, copied["oT"])
                for j in range(HP):
                    last = nc.tensor.matmul(ps[:], wo[:, j, :], oT[:, j, :], start=j == 0, stop=j == HP - 1)
                last.then_inc(f_full, 1)

            def ffn_in(it):
                ps = bank_f()
                pe.wait_ge(xs2_done, 2 * (it + 1))
                for t in range(NT):
                    last = nc.tensor.transpose(ps[:, 128 * t:128 * t + 128], xs2[:, 128 * t:128 * t + 128], ident[:])
                last.then_inc(f_full, 1)

            def ffn_norm(it):
                ps = bank_t("xnT")
                pe.wait_ge(f_free, FF * it + 3)
                for t in range(NT):
                    last = nc.tensor.transpose(ps[:, 128 * t:128 * t + 128], xn[:, t, :], ident[:])
                last.then_inc(t_full, 1)

            def ffn_gates(it):
                pe.wait_ge(t_free, copied["xnT"])
                pe.wait_ge(ready["w1"], it + 1)
                for k, m in enumerate(FC):
                    c0 = FI + 128 * k
                    nc.tensor.matmul(bank_t(f"gate{k}")[0:m, :], w1[:, c0:c0 + m], xnT[:], start=True, stop=True).then_inc(t_full, 1)

            def ffn_values(it, k):
                c0, m = 128 * k, FC[k]
                pe.wait_ge(t_free, copied[f"gate{k}"])
                nc.tensor.matmul(bank_f()[0:m, :], w1[:, c0:c0 + m], xnT[:], start=True, stop=True).then_inc(f_full, 1)

            def ffn_out(it):
                ps = bank_f()
                pe.wait_ge(ready["w2"], it + 1)
                for k, m in enumerate(FC):
                    last = nc.tensor.matmul(ps[:], w2[0:m, k, :], hid[0:m, k, :], start=k == 0, stop=k == len(FC) - 1)
                last.then_inc(f_full, 1)

            project_qk(0, 0)
            project_v(0, 0, (0, 1, 2, 3))
            transpose_qk(0, 0, range(4))
            project_qk(0, 1)
            project_v(0, 1, (0, 1, 2, 3))

            def body(it, first, last):
                for s in range(8):
                    t, hh = s // 2, s % 2
                    n = 8 * it + s
                    proj = not (last and t + 2 >= NT)
                    scores(it, s)
                    if not (first and s == 0):
                        transpose_p(n - 1, (s - 1) % 2)
                    if hh == 0 and not (last and t + 1 >= NT):
                        if proj:
                            project_qk(it, t + 2, lambda j: transpose_qk(it, t + 1, [j]))
                        else:
                            transpose_qk(it, t + 1, range(4))
                    if not first and s == 3:
                        ffn_in(it - 1)
                    if proj and hh == 1:
                        project_v(it, t + 2, (0, 1))
                    if not first and s in (6, 7):
                        ffn_values(it - 1, 0 if s == 6 else 2)
                    if proj and hh == 1:
                        project_v(it, t + 2, (2, 3))
                    if not first:
                        if s == 4:
                            ffn_norm(it - 1)
                        if s == 5:
                            ffn_gates(it - 1)
                        if s == 6:
                            ffn_values(it - 1, 1)
                    if not (first and s == 0):
                        values(it if s else it - 1, (s - 1) % 8)
                    if not (first and s < 2):
                        transpose_o(n - 2, s % 2)
                    if not first and s == 1:
                        output_projection(it - 1)
                    if not first and s == 7:
                        ffn_out(it - 1)

            turns(pe, body, [up, ut, uf])
            it, n = NIT - 1, 8 * NIT
            transpose_p(n - 1, 1)
            values(it, 7)
            transpose_o(n - 2, 0)
            transpose_o(n - 1, 1)
            output_projection(it)
            ffn_in(it)
            ffn_norm(it)
            ffn_gates(it)
            for k in range(3):
                ffn_values(it, k)
            ffn_out(it)

        @block.scalar
        def _(act):
            up, ut = Uses(PROJ), Uses(TR)
            act.preload_act_table(ACT.Exp)
            act.sem_inc(p_free, 2)
            act.sem_inc(t_free, 2)

            def full_p():
                n, bank = up.next()
                act.wait_ge(p_full, n + 1)
                return ps_p[bank % 2]

            def full_t():
                n, bank = ut.next()
                act.wait_ge(t_full, n + 1)
                return ps_t[bank % 2]

            x = keep.xF

            def shift(it, t):
                it2, t2 = ahead(it, t)
                base = (it2 % B) * S + 128 * t2
                tiles = NT * it + t
                if not (isinstance(tiles, int) and tiles < NT):
                    act.wait_ge(p_full, 8 * (tiles - 3))
                nc.scalar.copy(xs[0:64, W + 128 * t2:W + 128 * t2 + 128], x[0:64, bass.ds(base, 128)]).then_inc(xs_done, 1)
                skip = 1 if t2 == 0 else 0
                nc.scalar.copy(xs[64:128, W + 128 * t2 + skip:W + 128 * t2 + 128],
                               x[64:128, bass.ds(base - 1 + skip, 128 - skip)]).then_inc(xs_done, 1)

            def shift2(it):
                act.wait_ge(f_free, FF * it + 2)
                base = (it % B) * S
                nc.scalar.copy(xs2[0:64, :], x[0:64, bass.ds(base, S)]).then_inc(xs2_done, 1)
                nc.scalar.copy(xs2[64:128, 1:S], x[64:128, bass.ds(base, S - 1)]).then_inc(xs2_done, 1)

            def take_qk(it, t, after=lambda j: None):
                tiles = NT * it + t
                if not (isinstance(tiles, int) and tiles == 0):
                    act.wait_ge(cos_done, tiles)
                    act.wait_ge(sin_done, 2 * tiles)
                for j in range(4):
                    nc.scalar.copy(qk[:, 8 * j:8 * j + 8, :], full_p()[:].rearrange("p (h d) -> p h d", d=DH)).then_inc(p_free, 1)
                    after(j)
                act.wait_ge(p_free, 2 + 8 * tiles + 4)
                nc.scalar.activation(sq[:], qk[:], ACT.Square).then_inc(sq_done, 1)

            def take_v(it, t, windows):
                _, t2 = ahead(it, t)
                for w in windows:
                    nc.scalar.copy(V[:, 4 * t2 + w, :, 0:DH], full_p()[:].rearrange("p (h d) -> p h d", d=DH)).then_inc(p_free, 1)

            def take_qkT(it, t, parts):
                _, t2 = ahead(it, t)
                for j in parts:
                    src = full_t()[:].rearrange("p (j q) -> p j q", j=4)
                    dst, c0 = (qT, 0) if j < 2 else (kT, W)
                    nc.scalar.copy(dst[:, 4 * (j % 2):4 * (j % 2) + 4, c0 + 128 * t2:c0 + 128 * t2 + 128], src).then_inc(t_free, 1)

            def exps(n, bank):
                act.wait_ge(sub_done, n + 1)
                nc.scalar.activation(P[:, bank], P[:, bank], ACT.Exp, scale=QK_SCALE).then_inc(exp_done, 1)

            def take_PT(n, bank):
                ps = full_t()
                if not (isinstance(n, int) and n < 2):
                    act.wait_ge(pv_done, n - 1)
                nc.scalar.copy(PT[:, bank], ps[:].rearrange("p (j q) -> p j q", j=4)).then_inc(t_free, 1)

            def take_oT(s):
                t, hh = s // 2, s % 2
                nc.scalar.copy(oT[:, 4 * hh:4 * hh + 4, 128 * t:128 * t + 128],
                               full_t()[:].rearrange("p (j q) -> p j q", j=4)).then_inc(t_free, 1)

            def take_xnT(it):
                ps = full_t()
                act.wait_ge(ready["cols"], it + 1)
                nc.scalar.activation(xnT[:], ps[:], ACT.Identity, bias=cols[:, 1:2], scale=cols[:, 0:1]).then_inc(t_free, 1)

            def gates(it):
                for k, m in enumerate(FC):
                    nc.scalar.activation(gate[0:m, k, :], full_t()[0:m, :], ACT.Gelu, bias=cols[0:m, 6 + k:7 + k]).then_inc(t_free, 1)

            act.wait_ge(s_init, 4)
            for t in range(3):
                shift(0, t)
            take_qk(0, 0)
            take_v(0, 0, (0, 1, 2, 3))
            take_qkT(0, 0, range(4))
            take_qk(0, 1)
            take_v(0, 1, (0, 1, 2, 3))

            def body(it, first, last):
                for s in range(8):
                    t, hh = s // 2, s % 2
                    n = 8 * it + s
                    proj = not (last and t + 2 >= NT)
                    if not (first and s == 0):
                        take_PT(n - 1, (s - 1) % 2)
                    if hh == 0 and not (last and t + 1 >= NT):
                        if proj:
                            take_qk(it, t + 2, lambda j: take_qkT(it, t + 1, [j]))
                        else:
                            take_qkT(it, t + 1, range(4))
                    if proj and hh == 1:
                        take_v(it, t + 2, (0, 1))
                    if proj and hh == 1:
                        take_v(it, t + 2, (2, 3))
                    exps(n, s % 2)
                    if not first and s == 2:
                        shift2(it - 1)
                    if not first:
                        if s == 4:
                            take_xnT(it - 1)
                        if s == 5:
                            gates(it - 1)
                    if hh == 1 and not (last and t + 3 >= NT):
                        shift(it, t + 3)
                    if not (first and s < 2):
                        take_oT((s - 2) % 8)

            turns(act, body, [up, ut])
            take_PT(8 * NIT - 1, 1)
            take_oT(6)
            take_oT(7)
            shift2(NIT - 1)
            take_xnT(NIT - 1)
            gates(NIT - 1)

        @block.vector
        def _(dve):
            uf = Uses(FF)
            dve.sem_inc(f_free, 1)
            dve.wait_ge(s_c, 32)
            nc.vector.tensor_copy(ident_b[:], keep.ident[:]).then_inc(s_initv, 1)
            for k in range(2):
                nc.vector.tensor_copy(mask[:, k], mask_f[:, k:k + 1, :].broadcast_to([128, 8, 2 * W])).then_inc(s_initv, 1)
            x = keep.xF

            def full_f():
                n, _ = uf.next()
                dve.wait_ge(f_full, n + 1)
                return ps_f

            def maxima(it, s):
                n = 8 * it + s
                dve.wait_ge(s_full, n + 1)
                nc.vector.tensor_reduce(ss_max[:], ps_s[:], AX.X, ALU.max).then_inc(max_done, 1)
                dve.wait_ge(max_done, n + 1)
                nc.vector.tensor_tensor(P[:, s % 2], ps_s[:], ss_max[:].rearrange("p (h o) -> p h o", o=1).broadcast_to([128, 8, 2 * W]),
                                        ALU.subtract).then_inc(sub_done, 1)

            def norms_and_cos(it, t):
                tiles = NT * it + t
                dve.wait_ge(sq_done, tiles + 1)
                nc.vector.tensor_reduce(ss[:], sq[:], AX.X, ALU.add).then_inc(ss_done, 1)
                dve.wait_ge(ss_done, tiles + 1)
                nc.vector.tensor_scalar(ss[:], ss[:], 1e-24, None, ALU.max).then_inc(rm_done, 1)
                dve.wait_ge(tab_made, tiles + 1)
                if not (isinstance(tiles, int) and tiles == 0):
                    dve.wait_ge(rope_done, tiles)
                nc.vector.tensor_tensor(rcos[:].rearrange("p (k h) d -> p k h d", k=2), qk[:].rearrange("p (k h) d -> p k h d", k=2),
                                        st[:, 0:2 * DH].rearrange("p (k o d) -> p k o d", k=2, o=1).broadcast_to([128, 2, H, DH]),
                                        ALU.mult).then_inc(cos_done, 1)

            def rotate(it, t):
                tiles = NT * it + t
                dve.wait_ge(sin_done, 2 * (tiles + 1))
                dve.wait_ge(cos_done, tiles + 1)
                nc.vector.tensor_tensor(rcos[:], rcos[:], rsin[:], ALU.add).then_inc(sum_done, 1)
                dve.wait_ge(sum_done, tiles + 1)
                dve.wait_ge(rn_done, tiles + 1)
                nc.vector.tensor_tensor(rot[:], rcos[:], rn[:].rearrange("p (h o) -> p h o", o=1).broadcast_to([128, 2 * H, DH]),
                                        ALU.mult).then_inc(rope_done, 1)

            def divide(n, bank):
                dve.wait_ge(pv_done, n + 1)
                v = ps_o[:, :, 0:4 * (DH + 1)].rearrange("p e (j d) -> p e j d", j=4)
                nc.vector.reciprocal(rden[:], v[:, :, :, DH]).then_inc(rden_done, 1)
                dve.wait_ge(rden_done, n + 1)
                nc.vector.tensor_tensor(o[:, bank].rearrange("p j e d -> p e j d"), v[:, :, :, 0:DH],
                                        rden[:].rearrange("p e (j o) -> p e j o", o=1).broadcast_to([128, 2, 4, DH]),
                                        ALU.mult).then_inc(o_done, 1)

            def residual(it):
                ps = full_f()
                cur = x[:, bass.ds((it % B) * S, S)]
                nc.vector.tensor_tensor(cur, ps[:], cur, ALU.add).then_inc(f_free, 1)

            def norm_stats(it):
                ps = full_f()
                for t in range(NT):
                    nc.vector.bn_stats(stats[:, t, :], ps[:, 128 * t:128 * t + 128]).then_inc(st_done, 1)
                dve.wait_ge(st_done, NT * (it + 1))
                dve.sem_inc(aggr_begun, 1)
                for t in range(NT):
                    nc.vector.bn_aggr(mv[:, t, :], stats[:, t, :]).then_inc(mv_done, 1)
                dve.wait_ge(mv_done, NT * (it + 1))
                nc.vector.tensor_scalar(mv[:, :, 1], mv[:, :, 1], EPS, None, ALU.add).then_inc(var_done, 1)

            def norm(it):
                dve.wait_ge(rstd_done, it + 1)
                for t in range(NT):
                    last = nc.vector.tensor_scalar(xn[:, t, :], ps_f[:, 128 * t:128 * t + 128], mv[:, t, 0:1], rstd[:, t:t + 1],
                                                   ALU.subtract, ALU.mult)
                last.then_inc(f_free, 1)

            def hidden(it, k):
                m = FC[k]
                ps = full_f()
                nc.vector.scalar_tensor_tensor(hid[0:m, k, :], ps[0:m, :], cols[0:m, 3 + k:4 + k], gate[0:m, k, :],
                                               ALU.add, ALU.mult).then_inc(f_free, 1)

            def ffn_residual(it):
                ps = full_f()
                cur = x[:, bass.ds((it % B) * S, S)]
                nc.vector.scalar_tensor_tensor(cur, ps[:], cols[:, 2:3], cur, ALU.add, ALU.add).then_inc(f_free, 1)

            for t in range(2):
                norms_and_cos(0, t)
                rotate(0, t)

            def body(it, first, last):
                for s in range(8):
                    t, hh = s // 2, s % 2
                    n = 8 * it + s
                    proj = not (last and t + 2 >= NT)
                    maxima(it, s)
                    if not first and s == 2:
                        residual(it - 1)
                    if not first and s == 4:
                        norm(it - 1)
                    if not first and s in (6, 7):
                        hidden(it - 1, 0 if s == 6 else 2)
                    if proj and hh == 0:
                        norms_and_cos(it, t + 2)
                    if proj and hh == 1:
                        rotate(it, t + 2)
                    if not first and s == 3:
                        norm_stats(it - 1)
                    if not first and s == 6:
                        hidden(it - 1, 1)
                    if not (first and s == 0):
                        divide(n - 1, (s - 1) % 2)
                    if not first and s == 7:
                        ffn_residual(it - 1)

            turns(dve, body, [uf])
            it = NIT - 1
            divide(8 * NIT - 1, 1)
            residual(it)
            norm_stats(it)
            norm(it)
            for k in range(3):
                hidden(it, k)
            ffn_residual(it)


def final_layernorm(nc, a, keep, out):
    with ExitStack() as c:
        y = c.enter_context(nc.sbuf_tensor("y_fin", [128, B * NT, D], F32))
        stats = c.enter_context(nc.sbuf_tensor("stats_c", [128, B * NT, 6], F32))
        mv = c.enter_context(nc.sbuf_tensor("mv_c", [128, B * NT, 2], F32))
        rstd = c.enter_context(nc.sbuf_tensor("rstd_c", [128, B * NT], F32))
        ps = [c.enter_context(nc.psum_tensor(f"ps_c{b}", [128, NT, D], F32)) for b in range(B)]
        s_t, s_y, s_st, s_mv, s_var, s_rstd, s_n, s_out = (c.enter_context(nc.semaphore(n)) for n in (
            "c_transposed", "c_summed", "c_stats", "c_mv", "c_var", "c_rstd", "c_normed", "c_stored"))
        block = c.enter_context(nc.Block())

        @block.tensor
        def _(pe):
            for b in range(B):
                for t in range(NT):
                    last = nc.tensor.transpose(ps[b][:, t, :], keep.xF[:, b * S + 128 * t:b * S + 128 * t + 128], keep.ident[:])
                last.then_inc(s_t, 1)

        @block.gpsimd
        def _(pool):
            for b in range(B):
                pool.wait_ge(s_var, b + 1)
                nc.gpsimd.tensor_tensor(rstd[:, NT * b:NT * b + NT], mv[:, NT * b:NT * b + NT, 1], keep.half[:, 0:NT],
                                        ALU.pow).then_inc(s_rstd, 1)

        @block.vector
        def _(dve):
            for b in range(B):
                tiles = slice(NT * b, NT * b + NT)
                dve.wait_ge(s_t, b + 1)
                nc.vector.tensor_tensor(y[:, tiles, :], ps[b][:], keep.x1[:, tiles, :], ALU.add).then_inc(s_y, 1)
                dve.wait_ge(s_y, b + 1)
                for t in range(NT * b, NT * b + NT):
                    nc.vector.bn_stats(stats[:, t, :], y[:, t, :]).then_inc(s_st, 1)
                dve.wait_ge(s_st, NT * (b + 1))
                for t in range(NT * b, NT * b + NT):
                    nc.vector.bn_aggr(mv[:, t, :], stats[:, t, :]).then_inc(s_mv, 1)
                dve.wait_ge(s_mv, NT * (b + 1))
                nc.vector.tensor_scalar(mv[:, tiles, 1], mv[:, tiles, 1], EPS, None, ALU.add).then_inc(s_var, 1)
                dve.wait_ge(s_rstd, b + 1)
                for t in range(NT * b, NT * b + NT):
                    nc.vector.tensor_scalar(y[:, t, :], y[:, t, :], mv[:, t, 0:1], rstd[:, t:t + 1],
                                            ALU.subtract, ALU.mult).then_inc(s_n, 1)

        @block.sync
        def _(sp):
            for b in range(B):
                sp.wait_ge(s_n, NT * (b + 1))
                sp.dma_start(out[b].rearrange("(t p) d -> p t d", p=128), y[:, NT * b:NT * b + NT, :]).then_inc(s_out, 16)
            sp.wait_ge(s_out, 16 * B)


class Kept:
    pass


def program(nc, a, out):
    with ExitStack() as c:
        keep = Kept()
        keep.ident = c.enter_context(nc.sbuf_tensor("ident", [128, 128], F32))
        keep.half = c.enter_context(nc.sbuf_tensor("minus_half", [128, 128], F32))
        keep.x1 = c.enter_context(nc.sbuf_tensor("x1", [128, B * NT, 128], F32))
        keep.xF = c.enter_context(nc.sbuf_tensor("xF", [128, B * S], F32))
        dense_attention(nc, a, keep)
        local_layers(nc, a, keep)
        final_layernorm(nc, a, keep, out)


def shape_constants():
    f = np.float32
    pos = np.arange(S, dtype=f)[:, None]
    ids = np.arange(D // 2, dtype=f)
    theta = (f(10000.0) ** (f(-2.0) * ids)).astype(f) / f(D // 2)
    r = (pos * theta[None, :]).astype(f)
    feat = dense_order()
    cos, sin = np.cos(r).T[feat // 2], np.sin(r).T[feat // 2]
    sin = np.where((feat % 2 == 0)[:, None], -sin, sin)
    rope_a = np.stack([cos, sin], 1).astype(f)
    half = np.arange(0, DH, 2, dtype=f)
    inv_freq = (f(1.0) / f(10000.0) ** (half / f(DH))).astype(f)
    t = np.arange(S, dtype=f)
    freqs = (t[:, None] * inv_freq[None, :]).astype(f)
    freqs = np.concatenate([freqs, freqs], -1)
    base = ((half + f(0.4 * DH)) / f(1.4 * DH)).astype(f)
    scale = (base[None, :] ** ((t - f(S // 2)) / f(W // 2))[:, None]).astype(f)
    scale = np.concatenate([scale, scale], -1)
    inv = (f(1.0) / scale).astype(f)
    cos, sin = np.cos(freqs), np.sin(freqs)
    sin = np.concatenate([-sin[:, :DH // 2], sin[:, DH // 2:]], -1)
    tab = np.stack([cos * scale, cos * inv, sin * scale, sin * inv], 1).astype(f)
    tab = tab.reshape(NT, 128, 4 * DH).transpose(1, 0, 2)
    i, j = np.arange(W)[:, None], np.arange(2 * W)[None, :]
    seen = (i <= j) & (j <= i + W)
    mask = np.where(seen, f(0), f(-1e30))
    other = np.tile(mask, (4, 1))
    first = other.copy()
    first[:W, :W] = -1e30
    mask = np.stack([first, other], 1).astype(f)
    return {"ident": np.eye(128, dtype=f), "rope": rope_a, "tab": tab, "mask": mask}


def dense_order():
    return np.arange(D).reshape(H, HD).T.reshape(-1)


def lay_out(v):
    v = {k: np.asarray(x) for k, x in v.items()}
    A, F = (lambda n: v["L0_attn_" + n]), (lambda n: v["L0_ffn_" + n])
    p = dense_order()
    o = {}
    o["x"] = A("x")
    o["wA"] = np.stack([np.concatenate([A("Wd_q_w"), A("Wd_kv_w")], 1), A("Wk_r_w")[:, p], A("Wk_r_w")[:, p ^ 1]], 1)
    qs = [A("Wu_q_w")[:, p], A("Wq_r_w")[:, p], A("Wq_r_w")[:, p ^ 1]]
    ks = [A("Wu_k_w")[:, p], A("Wu_v_w"), A("Wu_v_w")]
    o["wU"] = np.concatenate([np.stack(qs, 1), np.stack(ks, 1)], 0)
    o["wO"] = A("Wo_w")
    o["bcol"] = np.stack([np.concatenate([A("Wd_q_b"), A("Wd_kv_b")]), A("Wu_q_b")[p], A("Wq_r_b")[p], A("Wq_r_b")[p ^ 1],
                          A("Wu_k_b")[p], A("Wk_r_b")[p], A("Wk_r_b")[p ^ 1]], 1)
    o["brow"] = np.stack([A("Wu_v_b"), A("Wo_b")], 0)
    qkv = F("Wqkv")
    o["wqk"] = qkv[:, :, :2 * H * DH]
    o["wv"] = qkv[:, :, 2 * H * DH:].reshape(DEPTH, D, 4, 2, 2, DH).transpose(0, 1, 3, 4, 2, 5).reshape(DEPTH, D, H * DH)
    o["wo"] = F("Wo").reshape(DEPTH, 4, 2, 2, DH, D).transpose(0, 2, 4, 3, 1, 5).reshape(DEPTH, 128, HP, D)
    o["w1"] = F("W1")
    w2 = np.zeros((DEPTH, 128 * len(FC), D), np.float32)
    w2[:, :FI] = F("W2")
    o["w2"] = w2.reshape(DEPTH, len(FC), 128, D).transpose(0, 2, 1, 3)
    cols = np.zeros((DEPTH, 9, 128), np.float32)
    cols[:, 0], cols[:, 1], cols[:, 2] = F("ln_g"), F("ln_b"), F("b2")
    for k in range(2):
        padded = np.zeros((DEPTH, 384), np.float32)
        padded[:, :FI] = F("b1")[:, FI * k:FI * (k + 1)]
        cols[:, 3 + 3 * k:6 + 3 * k] = padded.reshape(DEPTH, 3, 128)
    o["cols"] = cols.transpose(0, 2, 1)
    q, k = F("q_scale"), F("k_scale")
    o["scales"] = np.stack([q, k, np.roll(q, DH // 2, -1), np.roll(k, DH // 2, -1)], 1)
    o.update(shape_constants())
    return {n: np.ascontiguousarray(x) for n, x in o.items()}


def kernel(**inputs):
    import concourse.bacc as bacc
    from concourse.bass_utils import run_bass_kernel_spmd

    nc = bacc.Bacc("TRN2", target_bir_lowering=False, num_devices=1)
    arrays = lay_out(inputs)
    aps = {n: nc.dram_tensor("in_" + n, x.shape, mybir.dt.from_np(x.dtype), kind="ExternalInput").ap() for n, x in arrays.items()}
    out = nc.dram_tensor("y_out", (B, S, D), F32, kind="ExternalOutput").ap()
    program(nc, aps, out)
    r = run_bass_kernel_spmd(nc, [{"in_" + n: x for n, x in arrays.items()}], core_ids=[0])
    return r.results[0]["y_out"]
```

```python
from contextlib import ExitStack

import numpy as np
import concourse.bass as bass
from concourse import mybir

F32 = mybir.dt.float32
BF16 = mybir.dt.bfloat16
ACT = mybir.ActivationFunctionType
ALU = mybir.AluOpType
AX = mybir.AxisListType

B, S, D = 4, 512, 128
NT = S // 128
H = 16
HD = D // H
LAT = 64
SCORE_SCALE = 1.0 / float(np.sqrt(np.float32(H + LAT + LAT)))
DEPTH = 6
DH = 64
HP = H // 2
W = 32
QK_SCALE = 8.0
FI = int(D * 4 * 2 / 3)
FC = [min(128, FI - c) for c in range(0, FI, 128)]
EPS = 1e-5
NIT = DEPTH * B
TERMS = 9
ROWS = TERMS * HD


class Uses:

    def __init__(self, per_turn):
        self.per_turn, self.n, self.in_loop = per_turn, 0, 0

    def enter_loop(self, turn):
        self.in_loop, self.entered = turn * self.per_turn, self.n

    def leave_loop(self, turns):
        assert self.n == self.entered + self.per_turn
        self.n, self.in_loop = self.entered + turns * self.per_turn, 0

    def now(self):
        return self.in_loop + self.n

    def next(self):
        n = self.n
        self.n += 1
        return self.in_loop + n, n


def dense_attention(nc, a, keep):
    q_parts = nc.dram_tensor("q_parts", [B, 3, HD, H, S], BF16, kind="Internal").ap()
    k_parts = nc.dram_tensor("k_parts", [B, 3, HD, H, S], BF16, kind="Internal").ap()
    m_parts = nc.dram_tensor("m_parts", [3, H * NT, 128], BF16, kind="Internal").ap()
    with ExitStack() as c:
        def sb(name, shape, dt=F32):
            return c.enter_context(nc.sbuf_tensor(name, shape, dt))

        def sem(name):
            return c.enter_context(nc.semaphore(name))

        wA = sb("wA", [128, 3, 128])
        wU = sb("wU", [128, 3, 128])
        wO = sb("wO", [128, 128])
        bcol = sb("bcol", [128, 7])
        brow = sb("brow", [128, 2, 128])
        rope = sb("rope", [128, 2, S])
        x_b = sb("x_b", [128, NT, 128])
        x_r = sb("x_r", [128, NT, 128])
        xT = sb("xT", [128, S])
        lat = sb("lat", [128, S])
        t_cos = sb("t_cos", [128, S])
        t_sin = sb("t_sin", [128, S])
        qk_f = sb("qk_f", [128, 2, S])
        rest = sb("rest", [128, S])
        part = sb("part", [128, 2, 3, S], BF16)
        Q9 = sb("Q9", [ROWS + 3, H, S], BF16)
        K9 = sb("K9", [ROWS + 3, H, S], BF16)
        V = sb("V", [128, NT, H, 32])
        v_next = sb("v_next", [128, NT, H, HD])
        negmax = sb("negmax", [128, H, NT])
        nm_rest = sb("nm_rest", [4 * NT, 128])
        nm_part = sb("nm_part", [4 * NT, 3, 128], BF16)
        P = sb("P", [128, 2, 4, NT, S])
        pv_sb = sb("pv_sb", [128, S])
        rden = sb("rden", [128, NT, 4])
        o_t = sb("o_t", [128, NT, H, HD])
        oT = sb("oT_a", [128, S])
        y = sb("y", [128, NT, 128])
        stats = sb("stats_a", [128, NT, 6])
        mv = sb("mv_a", [128, NT, 2])
        rstd = sb("rstd_a", [128, NT])
        DB = 4
        ps_d = [c.enter_context(nc.psum_tensor(f"ps_d{i}", [128, S], F32)) for i in range(DB)]
        ps_a = [c.enter_context(nc.psum_tensor(f"ps_a{i}", [128, S], F32)) for i in range(2)]
        ps_pv = c.enter_context(nc.psum_tensor("ps_pv", [128, S], F32))
        ps_m = c.enter_context(nc.psum_tensor("ps_m", [128, S], F32))

        s_w = sem("a_weights")
        s_x = sem("a_x_loaded")
        s_const = sem("a_const")
        d_full, d_free = sem("ps_d_full"), sem("ps_d_free")
        a_full, a_free = sem("ps_a_full"), sem("ps_a_free")
        pv_full, pv_free = sem("ps_pv_full"), sem("ps_pv_free")
        m_full, m_free = sem("ps_m_full"), sem("ps_m_free")
        s_ident, s_wp = sem("a_ident_loaded"), sem("a_projections_loaded")
        s_dve = sem("a_dve_chain")
        s_qk = sem("a_qk_rotated")
        s_part = sem("a_parts_split")
        s_rest = sem("a_split_chain")
        s_scored = sem("a_group_scored")
        s_waited = sem("a_waits_carried")
        s_scr = [sem(f"a_parts_in_dram{k}") for k in range(2)]
        s_stack = [sem(f"a_stacked{g}") for g in range(H // 4)]
        s_nmp = sem("a_negmax_split")
        s_nscr = sem("a_negmax_in_dram")
        s_nrow = [sem(f"a_negmax_rows{g}") for g in range(H // 4)]
        s_vnext, s_v = sem("a_v_projected"), sem("a_v_in_place")
        s_xr = sem("a_x_reloaded")
        s_x1 = sem("a_x1_kept")
        s_stats, s_aggr, s_mv = sem("a_stats_done"), sem("a_aggr_begun"), sem("a_mv_done")
        s_var = sem("a_var_done")
        s_rstd = sem("a_rstd_done")
        s_y = sem("a_y_normalised")

        G = H // 4
        ND, NA, NM = 7 + H * NT + 1, 2 + 4 * H + 2, 2 * G
        CH = 2 + 2 * G + G + 1
        block = c.enter_context(nc.Block())

        def turns(engine, body, counters):
            body(0, False, True, True)
            with engine.Fori(1, B - 1) as b:
                for u in counters:
                    u.enter_loop(b - 1)
                body(b, True, True, True)
            for u in counters:
                u.leave_loop(B - 2)
            body(B - 1, True, True, False)
            body(B, True, False, False)

        def split(engine, ops, b, k):
            engine.wait_ge(s_qk, 2 * b + k + 1)
            if not (isinstance(b, int) and b == 0):
                engine.wait_ge(s_scr[k], 16 * b)
            done = 3 * (2 * b + k)
            engine.sem_inc(s_waited, 1)
            ops.tensor_copy(part[:, k, 0, :], qk_f[:, k, :]).then_inc(s_rest, 1)
            engine.wait_ge(s_rest, done + 1)
            ops.tensor_tensor(rest[:], qk_f[:, k, :], part[:, k, 0, :], ALU.subtract).then_inc(s_rest, 1)
            engine.wait_ge(s_rest, done + 2)
            engine.sem_inc(s_waited, 1)
            ops.tensor_copy(part[:, k, 1, :], rest[:]).then_inc(s_rest, 1)
            engine.wait_ge(s_rest, done + 3)
            ops.tensor_tensor(part[:, k, 2, :], rest[:], part[:, k, 1, :], ALU.subtract).then_inc(s_part, 1)

        values_at = (1, 2, 4, 5)

        def group(b, g, back):
            return b + (g - back) // G, (g - back) % G

        @block.sync
        def _(sp):
            def load_x(b, dst, done):
                sp.dma_start(dst[:], a["x"][bass.ds(b, 1), :, :].rearrange("o (t p) d -> p (o t) d", p=128)).then_inc(done, 16)

            def store_parts(b, k):
                sp.wait_ge(s_part, 2 * b + k + 1)
                scr = (q_parts, k_parts)[k]
                sp.dma_start(scr[bass.ds(b, 1)].rearrange("o a d h s -> (o d h) a s"), part[:, k]).then_inc(s_scr[k], 16)

            def stack(b, g):
                h = slice(4 * g, 4 * g + 4)
                if g == 0:
                    for k in range(2):
                        sp.wait_ge(s_scr[k], 16 * (b + 1))
                if not (isinstance(b, int) and b == 0):
                    sp.wait_ge(s_scored, G * (b - 1) + g + 1)
                for pa in range(3):
                    src = q_parts[bass.ds(b, 1), pa, :, h, :].rearrange("o d h s -> o d (h s)").broadcast_to([3, HD, 4 * S])
                    sp.dma_start(Q9[24 * pa:24 * pa + 24, h, :], src).then_inc(s_stack[g], 16)
                    src = k_parts[bass.ds(b, 1), :, :, h, :].rearrange("o b d h s -> (o b d) (h s)")
                    sp.dma_start(K9[24 * pa:24 * pa + 24, h, :], src).then_inc(s_stack[g], 16)

            def negmax_rows(b, g):
                sp.wait_ge(s_nmp, G * b + g + 1)
                sp.dma_start(m_parts[:, 16 * g:16 * g + 16, :].rearrange("a r q -> r a q"), nm_part[:]).then_inc(s_nscr, 16)
                sp.wait_ge(s_nscr, 16 * (G * b + g + 1))
                sp.dma_start(Q9[ROWS:ROWS + 3, 4 * g:4 * g + 4, :],
                             m_parts[:, 16 * g:16 * g + 16, :].rearrange("a (h t) q -> a h (t q)", h=4)).then_inc(s_nrow[g], 16)

            load_x(0, x_b, s_x)
            sp.dma_start(keep.ident[:], a["ident"]).then_inc(s_ident, 16)
            for dst, src in ((wA, a["wA"]), (bcol, a["bcol"]), (wU, a["wU"])):
                sp.dma_start(dst[:], src).then_inc(s_wp, 16)
            sp.dma_start(rope[:], a["rope"]).then_inc(s_w, 16)
            sp.dma_start(wO[:], a["wO"]).then_inc(s_w, 16)
            sp.dma_start(brow[:], a["brow"].rearrange("(o r) n -> o r n", o=1).broadcast_to([128, 2, 128])).then_inc(s_w, 16)
            store_parts(0, 0)
            store_parts(0, 1)
            sp.wait_ge(s_const, 4)
            stack(0, 0)

            def body(b, old, cur, new):
                for g in range(G):
                    if g == 0 and new:
                        sp.wait_ge(s_part, 2 * (b + 1))
                        load_x(b + 1, x_b, s_x)
                    if g < G - 1 and cur:
                        stack(b, g + 1)
                    if g == 0 and old:
                        negmax_rows(b - 1, G - 1)
                    if g > 0 and cur:
                        negmax_rows(b, g - 1)
                    if g in (1, 2) and new:
                        store_parts(b + 1, g - 1)
                    if g == 2 and old:
                        sp.wait_ge(s_stats, NT * (b - 1) + 1)
                        load_x(b - 1, x_r, s_xr)
                    if g == G - 1 and new:
                        stack(b + 1, 0)

            turns(sp, body, [])

        @block.gpsimd
        def _(pool):
            nc.gpsimd.memset(V[:], 0.0).then_inc(s_const, 1)
            nc.gpsimd.memset(K9[:], 1.0).then_inc(s_const, 1)
            nc.gpsimd.memset(keep.half[:], -0.5).then_inc(s_const, 1)
            pool.wait_ge(s_const, 3)
            nc.gpsimd.memset(V[:, :, :, HD:HD + 1], 1.0).then_inc(s_const, 1)
            pool.sem_inc(s_x1, 1)

            def body(b, old, cur, new):
                if new:
                    split(pool, nc.gpsimd, b + 1, 0)
                    split(pool, nc.gpsimd, b + 1, 1)
                if cur:
                    pool.wait_ge(s_vnext, b + 1)
                    if old:
                        pool.wait_ge(pv_full, G * b)
                    pool.sem_inc(s_waited, 1)
                    nc.gpsimd.tensor_copy(V[:, :, :, 0:HD], v_next[:]).then_inc(s_v, 1)
                if old:
                    pool.wait_ge(s_var, b)
                    nc.gpsimd.tensor_tensor(rstd[:], mv[:, :, 1], keep.half[:, 0:NT], ALU.pow).then_inc(s_rstd, 1)
                    pool.wait_ge(s_y, NT * b)
                    pool.sem_inc(s_waited, 1)
                    nc.gpsimd.tensor_copy(keep.x1[:, bass.ds((b - 1) * NT, NT), :], y[:]).then_inc(s_x1, 1)

            turns(pool, body, [])

        @block.tensor
        def _(pe):
            ud, ua, um = Uses(ND), Uses(NA), Uses(NM)

            def bank_d():
                n, bank = ud.next()
                pe.wait_ge(d_free, n + 1)
                return ps_d[bank % DB]

            def bank_a():
                n, bank = ua.next()
                pe.wait_ge(a_free, n + 1)
                return ps_a[bank % 2]

            def bank_m():
                n, _ = um.next()
                pe.wait_ge(m_free, n + 1)
                return ps_m

            ql, kl = slice(0, LAT), slice(LAT, 2 * LAT)

            def project_x(b):
                pe.wait_ge(s_x, 16 * (b + 1))
                ps = bank_a()
                for t in range(NT):
                    last = nc.tensor.transpose(ps[:, 128 * t:128 * t + 128], x_b[:, t, :], keep.ident[:])
                last.then_inc(a_full, 1)

            def project_latents():
                pe.wait_ge(a_free, ua.now() + 2)
                nc.tensor.matmul(bank_a()[:], wA[:, 0, :], xT[:], start=True, stop=True).then_inc(a_full, 1)
                return ua.now() + 2

            def project_q_or_k(k, n, copied):
                pe.wait_ge(a_free, copied)
                lhsT, rhs = (((wU[ql, 1, :], lat[ql, :]), (wU[ql, 2, :], lat[ql, :]), (wU[ql, 0, :], lat[ql, :])),
                                  ((wA[:, 1, :], xT[:]), (wA[:, 2, :], xT[:]), (wU[kl, 0, :], lat[kl, :])))[k][n]
                nc.tensor.matmul(bank_d()[:], lhsT, rhs, start=True, stop=True).then_inc(d_full, 1)

            def project_v():
                ps = bank_d()
                for t in range(NT):
                    last = nc.tensor.matmul(ps[:, 128 * t:128 * t + 128], lat[kl, 128 * t:128 * t + 128], wU[kl, 1, :],
                                            start=True, stop=True)
                last.then_inc(d_full, 1)

            def max_scores(h, tiles):
                for t in tiles:
                    nc.tensor.matmul(bank_d()[:], Q9[0:ROWS, h, 128 * t:128 * t + 128], K9[0:ROWS, h, :],
                                     start=True, stop=True).then_inc(d_full, 1)

            def exp_scores(h, t):
                nc.tensor.matmul(bank_a()[:], K9[:, h, 128 * t:128 * t + 128], Q9[:, h, :], start=True, stop=True).then_inc(a_full, 1)

            def transpose_negmax(g, written):
                pe.wait_ge(d_free, written)
                ps = bank_m()
                nc.tensor.transpose(ps[0:4 * NT, 0:128], negmax[:, 4 * g:4 * g + 4, :].rearrange("p h t -> p (h t)"),
                                    keep.ident[:]).then_inc(m_full, 1)

            def sum_values(b, g, t, written):
                if t == 0:
                    if g == 0:
                        pe.wait_ge(s_v, b + 1)
                    pe.wait_ge(pv_free, G * b + g + 1)
                    pe.wait_ge(a_free, written)
                    pe.sem_inc(s_scored, 1)
                for h in range(4):
                    last = nc.tensor.matmul(ps_pv[32 * h:32 * h + 32, :], V[:, t, 4 * g + h, :], P[:, g % 2, h, t, :],
                                            start=t == 0, stop=t == NT - 1, skip_group_check=True)
                if t == NT - 1:
                    last.then_inc(pv_full, 1)

            def transpose_values(b, g):
                ps = bank_m()
                pe.wait_ge(pv_free, G * b + g + 2)
                for t in range(NT):
                    last = nc.tensor.transpose(ps[:, 128 * t:128 * t + 128], pv_sb[:, 128 * t:128 * t + 128], keep.ident[:])
                last.then_inc(m_full, 1)

            def transpose_output():
                pe.wait_ge(m_free, um.now() + 1)
                ps = bank_a()
                for t in range(NT):
                    last = nc.tensor.transpose(ps[:, 128 * t:128 * t + 128], o_t[:, t].rearrange("p h d -> p (h d)"), keep.ident[:])
                last.then_inc(a_full, 1)
                return ua.now() + 2

            def project_output(copied):
                pe.wait_ge(a_free, copied)
                ps = bank_d()
                for t in range(NT):
                    last = nc.tensor.matmul(ps[:, 128 * t:128 * t + 128], oT[:, 128 * t:128 * t + 128], wO[:], start=True, stop=True)
                last.then_inc(d_full, 1)

            def transpose_y(b):
                pe.wait_ge(s_y, NT * (b + 1))
                ps = bank_a()
                for t in range(NT):
                    last = nc.tensor.transpose(ps[:, 128 * t:128 * t + 128], y[:, t, :], keep.ident[:])
                last.then_inc(a_full, 1)

            pe.wait_ge(s_ident, 16)
            project_x(0)
            pe.wait_ge(s_wp, 16 * 3)
            copied = project_latents()
            for k in range(2):
                for n in range(3):
                    project_q_or_k(k, n, copied)
            project_v()
            pe.wait_ge(s_const, 4)
            pe.wait_ge(s_w, 16 * 3)

            def body(b, old, cur, new):
                for g in range(G):
                    there = (old, cur)
                    exps, values, maxima_there = (there[g >= back] for back in (2, 3, 1))
                    (be, ge), (bv, gv), (_, gm) = (group(b, g, back) for back in (2, 3, 1))
                    maxima_written, exps_written = ud.now() + DB, ua.now() + 2
                    if cur:
                        pe.wait_ge(s_stack[g], 96 * (b + 1))
                    if exps:
                        pe.wait_ge(s_nrow[ge], 16 * (be + 1))
                    for j in range(8):
                        i, u = j // 2, j % 2
                        for t in (2 * u, 2 * u + 1):
                            if cur:
                                max_scores(4 * g + i, (t,))
                            if exps:
                                exp_scores(4 * ge + i, t)
                        if j == 2 and maxima_there:
                            transpose_negmax(gm, maxima_written)
                        if j in values_at and values:
                            sum_values(bv, gv, values_at.index(j), exps_written)
                        if new:
                            if (g, j) == (0, 0):
                                project_x(b + 1)
                            if (g, j) == (0, 2):
                                copied = project_latents()
                            if g < 2 and j >= 5:
                                project_q_or_k(g, j - 5, copied)
                            if (g, j) == (3, 7):
                                project_v()
                        if old:
                            if (g, j) == (3, 1):
                                output_copied = transpose_output()
                            if (g, j) == (3, 3):
                                project_output(output_copied)
                    if values:
                        transpose_values(bv, gv)
                if old:
                    transpose_y(b - 1)

            turns(pe, body, [ud, ua, um])

        @block.scalar
        def _(act):
            ua = Uses(NA)
            act.preload_act_table(ACT.Exp)
            act.sem_inc(a_free, 2)
            act.sem_inc(pv_free, 1)

            def full():
                n, bank = ua.next()
                act.wait_ge(a_full, n + 1)
                return ps_a[bank % 2]

            def take_x():
                nc.scalar.copy(xT[:], full()[:]).then_inc(a_free, 1)

            def take_latents():
                nc.scalar.activation(lat[:], full()[:], ACT.Identity, bias=bcol[:, 0:1]).then_inc(a_free, 1)

            take_x()
            act.wait_ge(s_wp, 16 * 3)
            take_latents()

            def body(b, old, cur, new):
                for g in range(G):
                    there = (old, cur)
                    exps, values = there[g >= 2], there[g >= 3]
                    (_, ge), (bv, gv) = group(b, g, 2), group(b, g, 3)
                    for j in range(8):
                        i, u = j // 2, j % 2
                        if exps:
                            for t in (2 * u, 2 * u + 1):
                                nc.scalar.activation(P[:, ge % 2, i, t, :], full()[:], ACT.Exp, scale=SCORE_SCALE).then_inc(a_free, 1)
                        if j == values_at[-1] and values:
                            act.wait_ge(pv_full, G * bv + gv + 1)
                            nc.scalar.copy(pv_sb[:], ps_pv[:]).then_inc(pv_free, 1)
                        if new:
                            if (g, j) == (0, 0):
                                take_x()
                            if (g, j) == (0, 2):
                                take_latents()
                        if old and (g, j) == (3, 1):
                            nc.scalar.copy(oT[:], full()[:]).then_inc(a_free, 1)
                if old:
                    nc.scalar.copy(keep.xF[:, bass.ds((b - 1) * S, S)], full()[:]).then_inc(a_free, 1)

            turns(act, body, [ua])

        @block.vector
        def _(dve):
            ud, um, chain = Uses(ND), Uses(NM), Uses(CH)
            dve.sem_inc(d_free, DB)
            dve.sem_inc(m_free, 1)
            dve.sem_inc(s_stats, 1)
            dve.wait_ge(s_wp, 16 * 3)
            dve.wait_ge(s_w, 16 * 3)

            def full():
                n, bank = ud.next()
                dve.wait_ge(d_full, n + 1)
                return ps_d[bank % DB]

            def full_m():
                n, _ = um.next()
                dve.wait_ge(m_full, n + 1)
                return ps_m

            def then(ins):
                n, _ = chain.next()
                ins.then_inc(s_dve, 1)
                dve.wait_ge(s_dve, n + 1)

            def rotate(b, k, n):
                bias = 1 + 3 * k
                if n < 2:
                    part_of = (t_cos, t_sin)[n]
                    nc.vector.scalar_tensor_tensor(part_of[:], full()[:], bcol[:, bias + 1 + n:bias + 2 + n], rope[:, n, :],
                                                   ALU.add, ALU.mult).then_inc(d_free, 1)
                if n == 1:
                    dve.wait_ge(d_free, ud.now() + DB)
                    then(nc.vector.tensor_tensor(t_cos[:], t_cos[:], t_sin[:], ALU.add))
                if n == 2:
                    if not (isinstance(b, int) and b == 0):
                        dve.wait_ge(s_part, 2 * (b - 1) + k + 1)
                    nc.vector.scalar_tensor_tensor(qk_f[:, k, :], full()[:], bcol[:, bias:bias + 1], t_cos[:], ALU.add, ALU.add).then_inc(d_free, 1)
                    dve.wait_ge(d_free, ud.now() + DB)
                    dve.sem_inc(s_qk, 1)

            def take_v(b):
                if not (isinstance(b, int) and b == 0):
                    dve.wait_ge(s_v, b)
                nc.vector.tensor_tensor(v_next[:], full()[:].rearrange("p (t h d) -> p t h d", t=NT, h=H),
                                        brow[:, 0:1, :].rearrange("p o (h d) -> p o h d", h=H).broadcast_to([128, NT, H, HD]),
                                        ALU.add).then_inc(d_free, 1)
                dve.wait_ge(d_free, ud.now() + DB)
                dve.sem_inc(s_vnext, 1)

            def maxima(h, tiles):
                for t in tiles:
                    nc.vector.tensor_reduce(negmax[:, h, t:t + 1], full()[:], AX.X, ALU.max, negate=True).then_inc(d_free, 1)

            def split_negmax(b, g):
                ps = full_m()
                if not (isinstance(b, int) and (b, g) == (0, 0)):
                    dve.wait_ge(s_nscr, 16 * (G * b + g))
                then(nc.vector.tensor_copy(nm_part[:, 0, :], ps[0:4 * NT, 0:128]))
                nc.vector.tensor_tensor(nm_rest[:], ps[0:4 * NT, 0:128], nm_part[:, 0, :], ALU.subtract).then_inc(m_free, 1)
                dve.wait_ge(m_free, um.now() + 1)
                then(nc.vector.tensor_copy(nm_part[:, 1, :], nm_rest[:]))
                nc.vector.tensor_tensor(nm_part[:, 2, :], nm_rest[:], nm_part[:, 1, :], ALU.subtract).then_inc(s_nmp, 1)

            def divide(g):
                ps = full_m()[:].rearrange("p (t h d) -> p t h d", t=NT, h=4)
                then(nc.vector.reciprocal(rden[:], ps[:, :, :, HD]))
                nc.vector.tensor_tensor(o_t[:, :, 4 * g:4 * g + 4, :], ps[:, :, :, 0:HD],
                                        rden[:].rearrange("p t (h o) -> p t h o", o=1).broadcast_to([128, NT, 4, HD]),
                                        ALU.mult).then_inc(m_free, 1)

            def residual(b):
                dve.wait_ge(s_xr, 16 * (b + 1))
                dve.wait_ge(s_x1, b + 1)
                nc.vector.tensor_tensor(y[:], full()[:].rearrange("p (t n) -> p t n", t=NT), x_r[:], ALU.add).then_inc(d_free, 1)
                dve.wait_ge(d_free, ud.now() + DB)
                then(nc.vector.tensor_tensor(y[:], y[:], brow[:, 1:2, :].broadcast_to([128, NT, 128]), ALU.add))

            def mean_and_variance(b):
                for t in range(NT):
                    nc.vector.bn_stats(stats[:, t, :], y[:, t, :]).then_inc(s_stats, 1)
                dve.wait_ge(s_stats, NT * (b + 1) + 1)
                dve.sem_inc(s_aggr, 1)
                for t in range(NT):
                    nc.vector.bn_aggr(mv[:, t, :], stats[:, t, :]).then_inc(s_mv, 1)
                dve.wait_ge(s_mv, NT * (b + 1))
                nc.vector.tensor_scalar(mv[:, :, 1], mv[:, :, 1], EPS, None, ALU.add).then_inc(s_var, 1)

            def normalise(b):
                dve.wait_ge(s_rstd, b + 1)
                for t in range(NT):
                    nc.vector.tensor_scalar(y[:, t, :], y[:, t, :], mv[:, t, 0:1], rstd[:, t:t + 1],
                                            ALU.subtract, ALU.mult).then_inc(s_y, 1)

            for k in range(2):
                for n in range(3):
                    rotate(0, k, n)
                split(dve, nc.vector, 0, k)
            take_v(0)

            def body(b, old, cur, new):
                for g in range(G):
                    there = (old, cur)
                    maxima_there, values = there[g >= 1], there[g >= 3]
                    (bm, gm), (_, gv) = group(b, g, 1), group(b, g, 3)
                    for j in range(8):
                        i, u = j // 2, j % 2
                        if cur:
                            maxima(4 * g + i, (2 * u, 2 * u + 1))
                        if j == 2 and maxima_there:
                            split_negmax(bm, gm)
                        if new:
                            if g < 2 and j >= 5:
                                rotate(b + 1, g, j - 5)
                            if (g, j) == (3, 7):
                                take_v(b + 1)
                        if old:
                            if (g, j) == (3, 3):
                                residual(b - 1)
                            if (g, j) == (3, 4):
                                mean_and_variance(b - 1)
                            if (g, j) == (3, 6):
                                normalise(b - 1)
                    if values:
                        divide(gv)

            turns(dve, body, [ud, um, chain])


def local_layers(nc, a, keep):
    with ExitStack() as c:
        def sb(name, shape, dt=F32):
            return c.enter_context(nc.sbuf_tensor(name, shape, dt))

        def sem(name):
            return c.enter_context(nc.semaphore(name))

        wqk = sb("wqk", [128, 2 * H * DH])
        wv = sb("wv", [128, 2, HP * DH])
        wo = sb("wo", [128, HP, D])
        w1 = sb("w1", [128, 2 * FI])
        w2 = sb("w2", [128, len(FC), D])
        cols = sb("cols", [128, 9])
        scales = sb("scales", [128, 4 * DH])
        tab = sb("tab", [128, NT, 4 * DH])
        mask_f = sb("mask_f", [128, 2, 2 * W])
        mask = sb("mask_bf", [128, 2, 8, 2 * W], BF16)
        ident_b = sb("ident_b", [128, 128], BF16)

        xs = sb("xs", [128, W + S])
        qk = sb("qk", [128, 2 * H, DH])
        sq = sb("sq", [128, 2 * H, DH])
        rcos = sb("rcos", [128, 2 * H, DH])
        rot = sb("rot", [128, 2 * H, DH])
        rsin = sb("rsin", [128, 2 * H, DH])
        ss = sb("ss", [128, 2 * H])
        rn = sb("rn", [128, 2 * H])
        st = sb("scaled_tab", [128, 4 * DH])
        qT = sb("qT", [128, HP, S])
        kT = sb("kT", [128, HP, W + S])
        V = sb("Vw", [128, S // W, HP, DH + 1])
        P = sb("Pl", [128, 2, 8, 2 * W])
        ss_max = sb("ss_max", [128, 8])
        PT = sb("PT", [128, 2, 4, 128])
        rden = sb("rden_l", [128, 2, 4])
        o = sb("o_l", [128, 2, 4, 2, DH])
        oT = sb("oT", [128, HP, S])
        xs2 = sb("xs2", [128, S])
        stats = sb("stats", [128, NT, 6])
        mv = sb("mv", [128, NT, 2])
        rstd = sb("rstd", [128, NT])
        xn = sb("xn", [128, NT, D])
        xnT = sb("xnT", [128, S])
        gate = sb("gate", [128, len(FC), S])
        hid = sb("hid", [128, len(FC), S])

        ps_p = [c.enter_context(nc.psum_tensor(f"ps_p{i}", [128, S], F32)) for i in range(2)]
        ps_t = [c.enter_context(nc.psum_tensor(f"ps_t{i}", [128, S], F32)) for i in range(2)]
        ps_s = c.enter_context(nc.psum_tensor("ps_s", [128, 8, 2 * W], F32))
        ps_o = c.enter_context(nc.psum_tensor("ps_o", [128, 2, S], F32))
        ps_f = c.enter_context(nc.psum_tensor("ps_f", [128, S], F32))

        s_c = sem("b_const_loaded")
        s_init = sem("b_init")
        s_initv = sem("b_init_vector")
        ld = {n: sem("ld_" + n) for n in ("wqk", "scales", "wv", "wo", "cols", "w1", "w2")}
        ready = {n: sem("ready_" + n) for n in ld}
        tab_made = sem("tab_made")
        p_full, p_free = sem("ps_p_full"), sem("ps_p_free")
        t_full, t_free = sem("ps_t_full"), sem("ps_t_free")
        f_full, f_free = sem("ps_f_full"), sem("ps_f_free")
        s_full, max_done, sub_done, exp_done = sem("scores_done"), sem("max_done"), sem("sub_done"), sem("exp_done")
        pv_done, rden_done, o_done = sem("pv_done"), sem("rden_done"), sem("o_done")
        xs_done = sem("xs_done")
        sq_done, ss_done, rm_done, rn_done = (sem(n) for n in ("sq_done", "ss_done", "rm_done", "rn_done"))
        sum_done, cos_done, sin_done, rope_done = sem("sum_done"), sem("cos_done"), sem("sin_done"), sem("rope_done")
        xs2_done = sem("xs2_done")
        values_begun, aggr_begun = sem("values_begun"), sem("aggr_begun")
        st_done, mv_done, var_done, rstd_done = sem("stats_done"), sem("mv_done"), sem("var_done"), sem("rstd_done")

        PROJ, TR, FF = 8 * NT, 16 + 8 + 8 + 1 + 3, 6
        block = c.enter_context(nc.Block())

        def turns(engine, body, counters):
            body(0, True, False)
            with engine.Fori(1, NIT - 1) as it:
                for u in counters:
                    u.enter_loop(it - 1)
                body(it, False, False)
            for u in counters:
                u.leave_loop(NIT - 2)
            body(NIT - 1, False, True)

        turn_about = ((), (0,), (1, 2), (3,))

        def ahead(it, t):
            return it + t // NT, t % NT

        @block.sync
        def _(sp):
            sp.dma_start(tab[:], a["tab"]).then_inc(s_c, 16)
            sp.dma_start(mask_f[:], a["mask"]).then_inc(s_c, 16)

            def src(n, layer):
                if n == "scales":
                    return a[n][bass.ds(layer, 1)].rearrange("o k d -> o (k d)").broadcast_to([128, 4 * DH])
                names = "o p " + " ".join("xyz"[:len(a[n].shape) - 2])
                return a[n][bass.ds(layer, 1)].rearrange(names + " -> p (o " + names[4:] + ")")

            def flat(x):
                return x[:] if len(x.shape) == 2 else x[:].rearrange("p a b -> p (a b)")

            dst = {"wqk": wqk, "scales": scales, "wv": wv, "wo": wo, "cols": cols, "w1": w1, "w2": w2}
            used = {"wqk": (p_full, PROJ * B, -4), "scales": (tab_made, NT * B, 0), "wv": (p_full, PROJ * B, 0),
                    "wo": (f_full, FF * B, 1 - FF), "cols": (f_free, FF * B, 1), "w1": (f_full, FF * B, 0), "w2": (f_full, FF * B, 0)}

            def load(layer, first):
                for group in (("wqk", "scales", "wv"), ("wo",), ("cols", "w1", "w2")):
                    for n in group:
                        if not first:
                            sem_used, per_layer, more = used[n]
                            sp.wait_ge(sem_used, layer * per_layer + more)
                        sp.dma_start(flat(dst[n]), src(n, layer)).then_inc(ld[n], 16)
                    for n in group:
                        sp.wait_ge(ld[n], 16 * (layer + 1))
                        sp.sem_inc(ready[n], B)

            load(0, True)
            with sp.Fori(1, DEPTH) as layer:
                load(layer, False)

        @block.gpsimd
        def _(pool):
            nc.gpsimd.memset(xs[:], 0.0).then_inc(s_init, 1)
            nc.gpsimd.memset(kT[:, :, 0:W], 0.0).then_inc(s_init, 1)
            nc.gpsimd.memset(V[:, :, :, DH:DH + 1], 1.0).then_inc(s_init, 1)
            pool.wait_ge(s_init, 3)
            pool.wait_ge(s_c, 32)

            def tables(it, t):
                it2, t2 = ahead(it, t)
                tiles = NT * it + t
                if t2 == 0:
                    pool.wait_ge(ready["scales"], it2 + 1)
                if not (isinstance(tiles, int) and tiles == 0):
                    pool.wait_ge(cos_done, tiles)
                    pool.wait_ge(sin_done, 2 * tiles)
                nc.gpsimd.tensor_tensor(st[:], tab[:, t2, :], scales[:], ALU.mult).then_inc(tab_made, 1)

            def sin_part(it, t):
                tiles = NT * it + t
                pool.wait_ge(p_free, 2 + 8 * tiles + 4)
                pool.wait_ge(tab_made, tiles + 1)
                if not (isinstance(tiles, int) and tiles == 0):
                    pool.wait_ge(sum_done, tiles)
                n4 = qk[:].rearrange("p (k h) (e d) -> p k h e d", k=2, e=2)
                r4 = rsin[:].rearrange("p (k h) (e d) -> p k h e d", k=2, e=2)
                sin = st[:, 2 * DH:4 * DH].rearrange("p (k o e d) -> p k o e d", k=2, o=1, e=2)
                for e in range(2):
                    nc.gpsimd.tensor_tensor(r4[:, :, :, e, :], n4[:, :, :, 1 - e, :],
                                            sin[:, :, :, e, :].broadcast_to([128, 2, H, DH // 2]), ALU.mult).then_inc(sin_done, 1)

            def inverse_norms(it, t):
                tiles = NT * it + t
                pool.wait_ge(rm_done, tiles + 1)
                nc.gpsimd.tensor_tensor(rn[:], ss[:], keep.half[:, 0:2 * H], ALU.pow).then_inc(rn_done, 1)

            def rstd_of(it):
                pool.wait_ge(var_done, it + 1)
                nc.gpsimd.tensor_tensor(rstd[:], mv[:, :, 1], keep.half[:, 0:NT], ALU.pow).then_inc(rstd_done, 1)

            nc.gpsimd.memset(xs2[:], 0.0).then_inc(s_init, 1)
            pool.wait_ge(s_init, 4)
            for t in range(2):
                tables(0, t)
                sin_part(0, t)
                inverse_norms(0, t)

            def body(it, first, last):
                for s in range(8):
                    t, hh = s // 2, s % 2
                    if hh == 0 and not (last and t + 2 >= NT):
                        tables(it, t + 2)
                        sin_part(it, t + 2)
                        inverse_norms(it, t + 2)
                    if s == 3 and not first:
                        rstd_of(it - 1)

            turns(pool, body, [])
            rstd_of(NIT - 1)

        @block.tensor
        def _(pe):
            up, ut, uf = Uses(PROJ), Uses(TR), Uses(FF)
            ident = keep.ident
            pe.wait_ge(s_init, 4)
            pe.wait_ge(s_initv, 3)

            def bank_p():
                n, bank = up.next()
                pe.wait_ge(p_free, n + 1)
                return ps_p[bank % 2]

            copied = {}

            def bank_t(what=None):
                n, bank = ut.next()
                pe.wait_ge(t_free, n + 1)
                copied[what] = n + 3
                return ps_t[bank % 2]

            def bank_f():
                n, _ = uf.next()
                pe.wait_ge(f_free, n + 1)
                return ps_f

            def project_qk(it, t, after=lambda j: None):
                it2, t2 = ahead(it, t)
                if t2 == 0:
                    pe.wait_ge(ready["wqk"], it2 + 1)
                pe.wait_ge(xs_done, 2 * (NT * it + t + 1))
                for j in range(4):
                    nc.tensor.matmul(bank_p()[:], xs[:, W + 128 * t2:W + 128 * t2 + 128], wqk[:, S * j:S * j + S],
                                     start=True, stop=True).then_inc(p_full, 1)
                    after(j)

            def project_v(it, t, windows):
                it2, t2 = ahead(it, t)
                if t2 == 0:
                    pe.wait_ge(ready["wv"], it2 + 1)
                for w in windows:
                    ps = bank_p()
                    for e in range(2):
                        last = nc.tensor.matmul(ps[64 * e:64 * e + 64, :], xs[:, 128 * t2 + W * w:128 * t2 + W * w + 2 * W],
                                                wv[:, e, :], start=True, stop=True, skip_group_check=True)
                    last.then_inc(p_full, 1)

            def transpose_qk(it, t, parts):
                pe.wait_ge(rope_done, NT * it + t + 1)
                flat = rot[:].rearrange("p h d -> p (h d)")
                for j in parts:
                    ps = bank_t()
                    for i in range(4):
                        last = nc.tensor.transpose(ps[:, 128 * i:128 * i + 128], flat[:, S * j + 128 * i:S * j + 128 * i + 128], ident[:])
                    last.then_inc(t_full, 1)

            def scores(it, s):
                t, hh = s // 2, s % 2
                n = 8 * it + s
                if not (isinstance(n, int) and n == 0):
                    pe.wait_ge(sub_done, n)
                nc.tensor.matmul(ps_s[:], ident_b[:], mask[:, 0 if t == 0 else 1, :, :], start=True, stop=False, skip_group_check=True)
                rows = slice(64 * hh, 64 * hh + 64)
                for j in range(8):
                    for w in range(4):
                        q0 = 128 * t + W * w
                        last = nc.tensor.matmul(ps_s[W * w:W * w + W, j, :], qT[rows, j, q0:q0 + W],
                                                kT[rows, j, q0:q0 + 2 * W], start=False, stop=True, skip_group_check=True)
                last.then_inc(s_full, 1)

            def transpose_p(n, bank):
                pe.wait_ge(exp_done, n + 1)
                ps = bank_t("PT")
                for j in range(4):
                    last = nc.tensor.transpose(ps[:, 128 * j:128 * j + 128], P[:, bank, 2 * j:2 * j + 2, :].rearrange("p e k -> p (e k)"), ident[:])
                last.then_inc(t_full, 1)

            def values(it, s):
                t, hh = s // 2, s % 2
                n = 8 * it + s
                pe.wait_ge(t_free, copied["PT"])
                pe.wait_ge(p_free, 2 + 8 * (NT * it + t + 1))
                if not (isinstance(n, int) and n == 0):
                    pe.wait_ge(o_done, n)
                pe.sem_inc(values_begun, 1)
                for j in range(4):
                    for e in range(2):
                        for w in range(4):
                            rows = slice(64 * e, 64 * e + 64)
                            last = nc.tensor.matmul(ps_o[W * w:W * w + W, e, (DH + 1) * j:(DH + 1) * (j + 1)],
                                                    PT[rows, s % 2, j, W * w:W * w + W], V[rows, 4 * t + w, 4 * hh + j, :],
                                                    start=True, stop=True, skip_group_check=True)
                last.then_inc(pv_done, 1)

            def transpose_o(n, bank):
                pe.wait_ge(o_done, n + 1)
                ps = bank_t("oT")
                for j in range(4):
                    last = nc.tensor.transpose(ps[:, 128 * j:128 * j + 128], o[:, bank, j, :, :].rearrange("p e d -> p (e d)"), ident[:])
                last.then_inc(t_full, 1)

            def output_projection(it):
                ps = bank_f()
                pe.wait_ge(ready["wo"], it + 1)
                pe.wait_ge(t_free, copied["oT"])
                for j in range(HP):
                    last = nc.tensor.matmul(ps[:], wo[:, j, :], oT[:, j, :], start=j == 0, stop=j == HP - 1)
                last.then_inc(f_full, 1)

            def ffn_in(it):
                ps = bank_f()
                pe.wait_ge(xs2_done, 2 * (it + 1))
                for t in range(NT):
                    last = nc.tensor.transpose(ps[:, 128 * t:128 * t + 128], xs2[:, 128 * t:128 * t + 128], ident[:])
                last.then_inc(f_full, 1)

            def ffn_norm(it):
                ps = bank_t("xnT")
                pe.wait_ge(f_free, FF * it + 3)
                for t in range(NT):
                    last = nc.tensor.transpose(ps[:, 128 * t:128 * t + 128], xn[:, t, :], ident[:])
                last.then_inc(t_full, 1)

            def ffn_gates(it, chunks):
                pe.wait_ge(t_free, copied["xnT"])
                pe.wait_ge(ready["w1"], it + 1)
                for k in chunks:
                    m, c0 = FC[k], FI + 128 * k
                    nc.tensor.matmul(bank_t(f"gate{k}")[0:m, :], w1[:, c0:c0 + m], xnT[:], start=True, stop=True).then_inc(t_full, 1)

            def ffn_values(it, k):
                c0, m = 128 * k, FC[k]
                pe.wait_ge(t_free, copied[f"gate{k}"])
                nc.tensor.matmul(bank_f()[0:m, :], w1[:, c0:c0 + m], xnT[:], start=True, stop=True).then_inc(f_full, 1)

            def ffn_out(it):
                ps = bank_f()
                pe.wait_ge(ready["w2"], it + 1)
                for k, m in enumerate(FC):
                    last = nc.tensor.matmul(ps[:], w2[0:m, k, :], hid[0:m, k, :], start=k == 0, stop=k == len(FC) - 1)
                last.then_inc(f_full, 1)

            project_qk(0, 0)
            project_v(0, 0, (0, 1, 2, 3))
            project_qk(0, 1)
            project_v(0, 1, (0, 1, 2, 3))
            transpose_qk(0, 0, range(4))
            pe.wait_ge(t_free, 2 + 4)

            def body(it, first, last):
                for s in range(8):
                    t, hh = s // 2, s % 2
                    n = 8 * it + s
                    proj = not (last and t + 2 >= NT)
                    scores(it, s)
                    if not (first and s == 0):
                        transpose_p(n - 1, (s - 1) % 2)
                    if not first and s == 6:
                        ffn_gates(it - 1, (2,))
                    if hh == 0 and not (last and t + 1 >= NT):
                        if proj:
                            project_qk(it, t + 2, lambda j: transpose_qk(it, t + 1, turn_about[j]))
                        else:
                            transpose_qk(it, t + 1, range(4))
                    if not first and s == 3:
                        ffn_in(it - 1)
                    if proj and hh == 1:
                        project_v(it, t + 2, (0, 1))
                    if not first and s in (6, 7):
                        ffn_values(it - 1, 0 if s == 6 else 2)
                    if proj and hh == 1:
                        project_v(it, t + 2, (2, 3))
                    if not first:
                        if s == 4:
                            ffn_norm(it - 1)
                    if not (first and s < 2):
                        transpose_o(n - 2, s % 2)
                    if not (first and s == 0):
                        values(it if s else it - 1, (s - 1) % 8)
                    if not first:
                        if s == 1:
                            output_projection(it - 1)
                        if s == 5:
                            ffn_gates(it - 1, (0, 1))
                        if s == 6:
                            ffn_values(it - 1, 1)
                    if not first and s == 7:
                        ffn_out(it - 1)

            turns(pe, body, [up, ut, uf])
            it, n = NIT - 1, 8 * NIT
            transpose_p(n - 1, 1)
            values(it, 7)
            transpose_o(n - 2, 0)
            transpose_o(n - 1, 1)
            output_projection(it)
            ffn_in(it)
            ffn_norm(it)
            ffn_gates(it, (0, 1, 2))
            for k in range(3):
                ffn_values(it, k)
            ffn_out(it)

        @block.scalar
        def _(act):
            up, ut = Uses(PROJ), Uses(TR)
            act.preload_act_table(ACT.Exp)
            act.sem_inc(p_free, 2)
            act.sem_inc(t_free, 2)

            def full_p():
                n, bank = up.next()
                act.wait_ge(p_full, n + 1)
                return ps_p[bank % 2]

            def full_t():
                n, bank = ut.next()
                act.wait_ge(t_full, n + 1)
                return ps_t[bank % 2]

            x = keep.xF

            def shift(it, t):
                it2, t2 = ahead(it, t)
                base = (it2 % B) * S + 128 * t2
                tiles = NT * it + t
                if not (isinstance(tiles, int) and tiles < NT):
                    act.wait_ge(p_full, 8 * (tiles - 3))
                nc.scalar.copy(xs[0:64, W + 128 * t2:W + 128 * t2 + 128], x[0:64, bass.ds(base, 128)]).then_inc(xs_done, 1)
                skip = 1 if t2 == 0 else 0
                nc.scalar.copy(xs[64:128, W + 128 * t2 + skip:W + 128 * t2 + 128],
                               x[64:128, bass.ds(base - 1 + skip, 128 - skip)]).then_inc(xs_done, 1)

            def shift2(it):
                act.wait_ge(f_free, FF * it + 2)
                base = (it % B) * S
                nc.scalar.copy(xs2[0:64, :], x[0:64, bass.ds(base, S)]).then_inc(xs2_done, 1)
                nc.scalar.copy(xs2[64:128, 1:S], x[64:128, bass.ds(base, S - 1)]).then_inc(xs2_done, 1)

            def take_qk(it, t, after=lambda j: None):
                tiles = NT * it + t
                if not (isinstance(tiles, int) and tiles == 0):
                    act.wait_ge(cos_done, tiles)
                    act.wait_ge(sin_done, 2 * tiles)
                for j in range(4):
                    nc.scalar.copy(qk[:, 8 * j:8 * j + 8, :], full_p()[:].rearrange("p (h d) -> p h d", d=DH)).then_inc(p_free, 1)
                    after(j)
                act.wait_ge(p_free, 2 + 8 * tiles + 4)
                nc.scalar.activation(sq[:], qk[:], ACT.Square).then_inc(sq_done, 1)

            def take_v(it, t, windows):
                _, t2 = ahead(it, t)
                for w in windows:
                    nc.scalar.copy(V[:, 4 * t2 + w, :, 0:DH], full_p()[:].rearrange("p (h d) -> p h d", d=DH)).then_inc(p_free, 1)

            def take_qkT(it, t, parts):
                _, t2 = ahead(it, t)
                for j in parts:
                    src = full_t()[:].rearrange("p (j q) -> p j q", j=4)
                    dst, c0 = (qT, 0) if j < 2 else (kT, W)
                    nc.scalar.copy(dst[:, 4 * (j % 2):4 * (j % 2) + 4, c0 + 128 * t2:c0 + 128 * t2 + 128], src).then_inc(t_free, 1)

            def exps(n, bank):
                act.wait_ge(sub_done, n + 1)
                nc.scalar.activation(P[:, bank], P[:, bank], ACT.Exp, scale=QK_SCALE).then_inc(exp_done, 1)

            def take_PT(n, bank):
                ps = full_t()
                if not (isinstance(n, int) and n < 2):
                    act.wait_ge(pv_done, n - 1)
                nc.scalar.copy(PT[:, bank], ps[:].rearrange("p (j q) -> p j q", j=4)).then_inc(t_free, 1)

            def take_oT(s):
                t, hh = s // 2, s % 2
                nc.scalar.copy(oT[:, 4 * hh:4 * hh + 4, 128 * t:128 * t + 128],
                               full_t()[:].rearrange("p (j q) -> p j q", j=4)).then_inc(t_free, 1)

            def take_xnT(it):
                ps = full_t()
                act.wait_ge(ready["cols"], it + 1)
                nc.scalar.activation(xnT[:], ps[:], ACT.Identity, bias=cols[:, 1:2], scale=cols[:, 0:1]).then_inc(t_free, 1)

            def gates(it, chunks):
                for k in chunks:
                    m = FC[k]
                    nc.scalar.activation(gate[0:m, k, :], full_t()[0:m, :], ACT.Gelu, bias=cols[0:m, 6 + k:7 + k]).then_inc(t_free, 1)

            act.wait_ge(s_init, 4)
            for t in range(3):
                shift(0, t)
            take_qk(0, 0)
            take_v(0, 0, (0, 1, 2, 3))
            take_qk(0, 1)
            take_v(0, 1, (0, 1, 2, 3))
            take_qkT(0, 0, range(4))

            def body(it, first, last):
                for s in range(8):
                    t, hh = s // 2, s % 2
                    n = 8 * it + s
                    proj = not (last and t + 2 >= NT)
                    if not (first and s == 0):
                        take_PT(n - 1, (s - 1) % 2)
                    if not first and s == 6:
                        gates(it - 1, (2,))
                    if hh == 0 and not (last and t + 1 >= NT):
                        if proj:
                            take_qk(it, t + 2, lambda j: take_qkT(it, t + 1, turn_about[j]))
                        else:
                            take_qkT(it, t + 1, range(4))
                    if proj and hh == 1:
                        take_v(it, t + 2, (0, 1))
                    if proj and hh == 1:
                        take_v(it, t + 2, (2, 3))
                    if hh == 1 and not (first and s == 1):
                        take_oT((s - 2) % 8)
                    exps(n, s % 2)
                    if not first and s == 2:
                        shift2(it - 1)
                    if not first:
                        if s == 4:
                            take_xnT(it - 1)
                    if hh == 1 and not (last and t + 3 >= NT):
                        shift(it, t + 3)
                    if hh == 0 and not (first and s == 0):
                        take_oT((s - 2) % 8)
                    if not first and s == 5:
                        gates(it - 1, (0, 1))

            turns(act, body, [up, ut])
            take_PT(8 * NIT - 1, 1)
            take_oT(6)
            take_oT(7)
            shift2(NIT - 1)
            take_xnT(NIT - 1)
            gates(NIT - 1, (0, 1, 2))

        @block.vector
        def _(dve):
            uf = Uses(FF)
            dve.sem_inc(f_free, 1)
            dve.wait_ge(s_c, 32)
            nc.vector.tensor_copy(ident_b[:], keep.ident[:]).then_inc(s_initv, 1)
            for k in range(2):
                nc.vector.tensor_copy(mask[:, k], mask_f[:, k:k + 1, :].broadcast_to([128, 8, 2 * W])).then_inc(s_initv, 1)
            x = keep.xF

            def full_f():
                n, _ = uf.next()
                dve.wait_ge(f_full, n + 1)
                return ps_f

            def maxima(it, s):
                n = 8 * it + s
                dve.wait_ge(s_full, n + 1)
                nc.vector.tensor_reduce(ss_max[:], ps_s[:], AX.X, ALU.max).then_inc(max_done, 1)
                dve.wait_ge(max_done, n + 1)
                nc.vector.tensor_tensor(P[:, s % 2], ps_s[:], ss_max[:].rearrange("p (h o) -> p h o", o=1).broadcast_to([128, 8, 2 * W]),
                                        ALU.subtract).then_inc(sub_done, 1)

            def norms(it, t):
                tiles = NT * it + t
                dve.wait_ge(sq_done, tiles + 1)
                nc.vector.tensor_reduce(ss[:], sq[:], AX.X, ALU.add).then_inc(ss_done, 1)
                dve.wait_ge(ss_done, tiles + 1)
                nc.vector.tensor_scalar(ss[:], ss[:], 1e-24, None, ALU.max).then_inc(rm_done, 1)

            def times_cos(it, t):
                tiles = NT * it + t
                dve.wait_ge(tab_made, tiles + 1)
                if not (isinstance(tiles, int) and tiles == 0):
                    dve.wait_ge(rope_done, tiles)
                nc.vector.tensor_tensor(rcos[:].rearrange("p (k h) d -> p k h d", k=2), qk[:].rearrange("p (k h) d -> p k h d", k=2),
                                        st[:, 0:2 * DH].rearrange("p (k o d) -> p k o d", k=2, o=1).broadcast_to([128, 2, H, DH]),
                                        ALU.mult).then_inc(cos_done, 1)

            def rotate(it, t):
                tiles = NT * it + t
                dve.wait_ge(sin_done, 2 * (tiles + 1))
                dve.wait_ge(cos_done, tiles + 1)
                nc.vector.tensor_tensor(rcos[:], rcos[:], rsin[:], ALU.add).then_inc(sum_done, 1)
                dve.wait_ge(sum_done, tiles + 1)
                dve.wait_ge(rn_done, tiles + 1)
                nc.vector.tensor_tensor(rot[:], rcos[:], rn[:].rearrange("p (h o) -> p h o", o=1).broadcast_to([128, 2 * H, DH]),
                                        ALU.mult).then_inc(rope_done, 1)

            def divide(n, bank):
                dve.wait_ge(pv_done, n + 1)
                v = ps_o[:, :, 0:4 * (DH + 1)].rearrange("p e (j d) -> p e j d", j=4)
                nc.vector.reciprocal(rden[:], v[:, :, :, DH]).then_inc(rden_done, 1)
                dve.wait_ge(rden_done, n + 1)
                nc.vector.tensor_tensor(o[:, bank].rearrange("p j e d -> p e j d"), v[:, :, :, 0:DH],
                                        rden[:].rearrange("p e (j o) -> p e j o", o=1).broadcast_to([128, 2, 4, DH]),
                                        ALU.mult).then_inc(o_done, 1)

            def residual(it):
                ps = full_f()
                cur = x[:, bass.ds((it % B) * S, S)]
                nc.vector.tensor_tensor(cur, ps[:], cur, ALU.add).then_inc(f_free, 1)

            def norm_stats(it):
                ps = full_f()
                for t in range(NT):
                    nc.vector.bn_stats(stats[:, t, :], ps[:, 128 * t:128 * t + 128]).then_inc(st_done, 1)
                dve.wait_ge(st_done, NT * (it + 1))
                dve.sem_inc(aggr_begun, 1)
                for t in range(NT):
                    nc.vector.bn_aggr(mv[:, t, :], stats[:, t, :]).then_inc(mv_done, 1)
                dve.wait_ge(mv_done, NT * (it + 1))
                nc.vector.tensor_scalar(mv[:, :, 1], mv[:, :, 1], EPS, None, ALU.add).then_inc(var_done, 1)

            def norm(it):
                dve.wait_ge(rstd_done, it + 1)
                for t in range(NT):
                    last = nc.vector.tensor_scalar(xn[:, t, :], ps_f[:, 128 * t:128 * t + 128], mv[:, t, 0:1], rstd[:, t:t + 1],
                                                   ALU.subtract, ALU.mult)
                last.then_inc(f_free, 1)

            def hidden(it, k):
                m = FC[k]
                ps = full_f()
                nc.vector.scalar_tensor_tensor(hid[0:m, k, :], ps[0:m, :], cols[0:m, 3 + k:4 + k], gate[0:m, k, :],
                                               ALU.add, ALU.mult).then_inc(f_free, 1)

            def ffn_residual(it):
                ps = full_f()
                cur = x[:, bass.ds((it % B) * S, S)]
                nc.vector.scalar_tensor_tensor(cur, ps[:], cols[:, 2:3], cur, ALU.add, ALU.add).then_inc(f_free, 1)

            for t in range(2):
                norms(0, t)
                times_cos(0, t)
                if t == 1:
                    dve.wait_ge(t_full, 4)
                rotate(0, t)

            def body(it, first, last):
                for s in range(8):
                    t, hh = s // 2, s % 2
                    n = 8 * it + s
                    proj = not (last and t + 2 >= NT)
                    maxima(it, s)
                    if not first and s == 2:
                        residual(it - 1)
                    if not first and s == 4:
                        norm(it - 1)
                    if not first and s in (6, 7):
                        hidden(it - 1, 0 if s == 6 else 2)
                    if proj and hh == 0:
                        norms(it, t + 2)
                    if proj and hh == 1:
                        times_cos(it, t + 2)
                        rotate(it, t + 2)
                    if not (first and s == 0):
                        divide(n - 1, (s - 1) % 2)
                    if not first and s == 6:
                        hidden(it - 1, 1)
                    if not first and s == 3:
                        norm_stats(it - 1)
                    if not first and s == 7:
                        ffn_residual(it - 1)

            turns(dve, body, [uf])
            it = NIT - 1
            divide(8 * NIT - 1, 1)
            residual(it)
            norm_stats(it)
            norm(it)
            for k in range(3):
                hidden(it, k)
            ffn_residual(it)


def final_layernorm(nc, a, keep, out):
    with ExitStack() as c:
        y = c.enter_context(nc.sbuf_tensor("y_fin", [128, B * NT, D], F32))
        stats = c.enter_context(nc.sbuf_tensor("stats_c", [128, B * NT, 6], F32))
        mv = c.enter_context(nc.sbuf_tensor("mv_c", [128, B * NT, 2], F32))
        rstd = c.enter_context(nc.sbuf_tensor("rstd_c", [128, B * NT], F32))
        ps = [c.enter_context(nc.psum_tensor(f"ps_c{b}", [128, NT, D], F32)) for b in range(B)]
        s_t, s_y, s_st, s_mv, s_var, s_rstd, s_n, s_out = (c.enter_context(nc.semaphore(n)) for n in (
            "c_transposed", "c_summed", "c_stats", "c_mv", "c_var", "c_rstd", "c_normed", "c_stored"))
        block = c.enter_context(nc.Block())

        @block.tensor
        def _(pe):
            for b in range(B):
                for t in range(NT):
                    last = nc.tensor.transpose(ps[b][:, t, :], keep.xF[:, b * S + 128 * t:b * S + 128 * t + 128], keep.ident[:])
                last.then_inc(s_t, 1)

        @block.gpsimd
        def _(pool):
            for b in range(B):
                pool.wait_ge(s_var, b + 1)
                nc.gpsimd.tensor_tensor(rstd[:, NT * b:NT * b + NT], mv[:, NT * b:NT * b + NT, 1], keep.half[:, 0:NT],
                                        ALU.pow).then_inc(s_rstd, 1)

        @block.vector
        def _(dve):
            for b in range(B):
                tiles = slice(NT * b, NT * b + NT)
                dve.wait_ge(s_t, b + 1)
                nc.vector.tensor_tensor(y[:, tiles, :], ps[b][:], keep.x1[:, tiles, :], ALU.add).then_inc(s_y, 1)
                dve.wait_ge(s_y, b + 1)
                for t in range(NT * b, NT * b + NT):
                    nc.vector.bn_stats(stats[:, t, :], y[:, t, :]).then_inc(s_st, 1)
                dve.wait_ge(s_st, NT * (b + 1))
                for t in range(NT * b, NT * b + NT):
                    nc.vector.bn_aggr(mv[:, t, :], stats[:, t, :]).then_inc(s_mv, 1)
                dve.wait_ge(s_mv, NT * (b + 1))
                nc.vector.tensor_scalar(mv[:, tiles, 1], mv[:, tiles, 1], EPS, None, ALU.add).then_inc(s_var, 1)
                dve.wait_ge(s_rstd, b + 1)
                for t in range(NT * b, NT * b + NT):
                    nc.vector.tensor_scalar(y[:, t, :], y[:, t, :], mv[:, t, 0:1], rstd[:, t:t + 1],
                                            ALU.subtract, ALU.mult).then_inc(s_n, 1)

        @block.sync
        def _(sp):
            for b in range(B):
                sp.wait_ge(s_n, NT * (b + 1))
                sp.dma_start(out[b].rearrange("(t p) d -> p t d", p=128), y[:, NT * b:NT * b + NT, :]).then_inc(s_out, 16)
            sp.wait_ge(s_out, 16 * B)


class Kept:
    pass


def program(nc, a, out):
    with ExitStack() as c:
        keep = Kept()
        keep.ident = c.enter_context(nc.sbuf_tensor("ident", [128, 128], F32))
        keep.half = c.enter_context(nc.sbuf_tensor("minus_half", [128, 128], F32))
        keep.x1 = c.enter_context(nc.sbuf_tensor("x1", [128, B * NT, 128], F32))
        keep.xF = c.enter_context(nc.sbuf_tensor("xF", [128, B * S], F32))
        dense_attention(nc, a, keep)
        local_layers(nc, a, keep)
        final_layernorm(nc, a, keep, out)


def shape_constants():
    f = np.float32
    pos = np.arange(S, dtype=f)[:, None]
    ids = np.arange(D // 2, dtype=f)
    theta = (f(10000.0) ** (f(-2.0) * ids)).astype(f) / f(D // 2)
    r = (pos * theta[None, :]).astype(f)
    feat = dense_order()
    cos, sin = np.cos(r).T[feat // 2], np.sin(r).T[feat // 2]
    sin = np.where((feat % 2 == 0)[:, None], -sin, sin)
    rope_a = np.stack([cos, sin], 1).astype(f)
    half = np.arange(0, DH, 2, dtype=f)
    inv_freq = (f(1.0) / f(10000.0) ** (half / f(DH))).astype(f)
    t = np.arange(S, dtype=f)
    freqs = (t[:, None] * inv_freq[None, :]).astype(f)
    freqs = np.concatenate([freqs, freqs], -1)
    base = ((half + f(0.4 * DH)) / f(1.4 * DH)).astype(f)
    scale = (base[None, :] ** ((t - f(S // 2)) / f(W // 2))[:, None]).astype(f)
    scale = np.concatenate([scale, scale], -1)
    inv = (f(1.0) / scale).astype(f)
    cos, sin = np.cos(freqs), np.sin(freqs)
    sin = np.concatenate([-sin[:, :DH // 2], sin[:, DH // 2:]], -1)
    tab = np.stack([cos * scale, cos * inv, sin * scale, sin * inv], 1).astype(f)
    tab = tab.reshape(NT, 128, 4 * DH).transpose(1, 0, 2)
    i, j = np.arange(W)[:, None], np.arange(2 * W)[None, :]
    seen = (i <= j) & (j <= i + W)
    mask = np.where(seen, f(0), f(-1e30))
    other = np.tile(mask, (4, 1))
    first = other.copy()
    first[:W, :W] = -1e30
    mask = np.stack([first, other], 1).astype(f)
    return {"ident": np.eye(128, dtype=f), "rope": rope_a, "tab": tab, "mask": mask}


def dense_order():
    return np.arange(D).reshape(H, HD).T.reshape(-1)


def lay_out(v):
    v = {k: np.asarray(x) for k, x in v.items()}
    A, F = (lambda n: v["L0_attn_" + n]), (lambda n: v["L0_ffn_" + n])
    p = dense_order()
    o = {}
    o["x"] = A("x")
    o["wA"] = np.stack([np.concatenate([A("Wd_q_w"), A("Wd_kv_w")], 1), A("Wk_r_w")[:, p], A("Wk_r_w")[:, p ^ 1]], 1)
    qs = [A("Wu_q_w")[:, p], A("Wq_r_w")[:, p], A("Wq_r_w")[:, p ^ 1]]
    ks = [A("Wu_k_w")[:, p], A("Wu_v_w"), A("Wu_v_w")]
    o["wU"] = np.concatenate([np.stack(qs, 1), np.stack(ks, 1)], 0)
    o["wO"] = A("Wo_w")
    o["bcol"] = np.stack([np.concatenate([A("Wd_q_b"), A("Wd_kv_b")]), A("Wu_q_b")[p], A("Wq_r_b")[p], A("Wq_r_b")[p ^ 1],
                          A("Wu_k_b")[p], A("Wk_r_b")[p], A("Wk_r_b")[p ^ 1]], 1)
    o["brow"] = np.stack([A("Wu_v_b"), A("Wo_b")], 0)
    qkv = F("Wqkv")
    o["wqk"] = qkv[:, :, :2 * H * DH]
    o["wv"] = qkv[:, :, 2 * H * DH:].reshape(DEPTH, D, 4, 2, 2, DH).transpose(0, 1, 3, 4, 2, 5).reshape(DEPTH, D, H * DH)
    o["wo"] = F("Wo").reshape(DEPTH, 4, 2, 2, DH, D).transpose(0, 2, 4, 3, 1, 5).reshape(DEPTH, 128, HP, D)
    o["w1"] = F("W1")
    w2 = np.zeros((DEPTH, 128 * len(FC), D), np.float32)
    w2[:, :FI] = F("W2")
    o["w2"] = w2.reshape(DEPTH, len(FC), 128, D).transpose(0, 2, 1, 3)
    cols = np.zeros((DEPTH, 9, 128), np.float32)
    cols[:, 0], cols[:, 1], cols[:, 2] = F("ln_g"), F("ln_b"), F("b2")
    for k in range(2):
        padded = np.zeros((DEPTH, 384), np.float32)
        padded[:, :FI] = F("b1")[:, FI * k:FI * (k + 1)]
        cols[:, 3 + 3 * k:6 + 3 * k] = padded.reshape(DEPTH, 3, 128)
    o["cols"] = cols.transpose(0, 2, 1)
    q, k = F("q_scale"), F("k_scale")
    o["scales"] = np.stack([q, k, np.roll(q, DH // 2, -1), np.roll(k, DH // 2, -1)], 1)
    o.update(shape_constants())
    return {n: np.ascontiguousarray(x) for n, x in o.items()}


def kernel(**inputs):
    import concourse.bacc as bacc
    from concourse.bass_utils import run_bass_kernel_spmd

    nc = bacc.Bacc("TRN2", target_bir_lowering=False, num_devices=1)
    arrays = lay_out(inputs)
    aps = {n: nc.dram_tensor("in_" + n, x.shape, mybir.dt.from_np(x.dtype), kind="ExternalInput").ap() for n, x in arrays.items()}
    out = nc.dram_tensor("y_out", (B, S, D), F32, kind="ExternalOutput").ap()
    program(nc, aps, out)
    r = run_bass_kernel_spmd(nc, [{"in_" + n: x for n, x in arrays.items()}], core_ids=[0])
    return r.results[0]["y_out"]
```
